# Optimizing a Trainium2 kernel written in Bass

```python
import numpy as np
import jax
import jax.numpy as jnp

def _softmax(x, axis=-1):
    return jax.nn.softmax(x, axis=axis)

def _gelu(x):
    return jax.nn.gelu(x, approximate=True)

def _silu(x):
    return jax.nn.silu(x)

def _sigmoid(x):
    return jax.nn.sigmoid(x)

def _layernorm(x, axis=-1, eps=1e-05):
    m = jnp.mean(x, axis=axis, keepdims=True)
    v = jnp.var(x, axis=axis, keepdims=True)
    return (x - m) / jnp.sqrt(v + eps)

def _scatter_add(tgt, idx, src, axis=0):
    return tgt.at[idx].add(src)

def _segment_sum(src, seg, n):
    return jax.ops.segment_sum(src, seg, n)
kernel_name = 'mk_adj_resnorm_d2_adj_r2_54deed'

def setup_inputs(seed: int=0):
    np.random.seed(seed)
    _w = jnp.asarray

    def _rec_inputs():
        import jax
        import jax.numpy as jnp
        _gk = jax.random.key(seed)
        x = 4.136e-05 + 0.9999 * jax.random.normal(jax.random.fold_in(_gk, 1), (4096, 256), jnp.float32)
        _a = jax.random.bernoulli(jax.random.fold_in(_gk, 2), 0.000976562, (4096, 4096))
        _a = jnp.logical_or(_a, jnp.swapaxes(_a, -1, -2))
        _a = jnp.logical_or(_a, jnp.eye(4096, dtype=bool))
        _af = _a.astype(jnp.float32)
        adj = _af
        return (x, adj)
    x, adj = _rec_inputs()

    def _L0_gnn_setup():
        import jax, jax.numpy as jnp
        import numpy as np
        N = 8192
        D_IN = 256
        D_OUT = 256
        AVG_DEG = 32.0
        key = jax.random.key(seed)
        k1, k2, k3, k4 = jax.random.split(key, 4)
        p = AVG_DEG / N
        adjacency = (jax.random.uniform(k1, (N, N)) < p).astype(jnp.float32)
        adjacency = jnp.maximum(adjacency, adjacency.T)
        node_degree = jnp.sum(adjacency, axis=1, keepdims=True) + 1.0
        x = jax.random.normal(k2, (N, D_IN), dtype=jnp.float32)
        W = jax.random.normal(k3, (D_IN, D_OUT), dtype=jnp.float32) * (1.0 / np.sqrt(D_IN))
        b = jax.random.normal(k4, (D_OUT,), dtype=jnp.float32) * 0.01
        return {'x': x, 'adjacency': adjacency, 'node_degree': node_degree, 'W': W, 'b': b}
    _L0_gnn_all = _L0_gnn_setup()
    _L0_gnn_in = {k: v for k, v in _L0_gnn_all.items() if k in ('W', 'b')}
    del _L0_gnn_all

    def _L1_gnn_setup():
        import jax, jax.numpy as jnp
        import numpy as np
        N = 3072
        D_IN = 256
        D_OUT = 256
        DENSITY = 0.005
        key = jax.random.key(seed)
        ks = jax.random.split(key, 12)
        x = jax.random.normal(ks[0], (N, D_IN), dtype=jnp.float32)
        adj_a = (jax.random.uniform(ks[1], (N, N)) < DENSITY).astype(jnp.float32)
        adj_b = (jax.random.uniform(ks[2], (N, N)) < DENSITY).astype(jnp.float32)
        W_sa = jax.random.normal(ks[3], (D_IN, D_OUT), dtype=jnp.float32) * (1.414 / np.sqrt(D_IN + D_OUT))
        a_sa = jax.random.normal(ks[4], (1, 2 * D_OUT), dtype=jnp.float32) * (1.414 / np.sqrt(1 + 2 * D_OUT))
        stdv = 1.0 / np.sqrt(D_OUT)
        W_gcnb = jax.random.uniform(ks[5], (D_IN, D_OUT), minval=-stdv, maxval=stdv, dtype=jnp.float32)
        b_gcnb = jax.random.uniform(ks[6], (D_OUT,), minval=-stdv, maxval=stdv, dtype=jnp.float32)
        s = 1.0 / np.sqrt(2 * D_IN)
        Wa = jax.random.uniform(ks[7], (1, 2 * D_IN), minval=-s, maxval=s, dtype=jnp.float32)
        ba = jax.random.uniform(ks[8], (1,), minval=-s, maxval=s, dtype=jnp.float32)
        Wb = jax.random.uniform(ks[9], (1, 2 * D_IN), minval=-s, maxval=s, dtype=jnp.float32)
        bb = jax.random.uniform(ks[10], (1,), minval=-s, maxval=s, dtype=jnp.float32)
        return {'x': x, 'adj_a': adj_a, 'adj_b': adj_b, 'W_sa': W_sa, 'a_sa': a_sa, 'W_gcnb': W_gcnb, 'b_gcnb': b_gcnb, 'Wa': Wa, 'ba': ba, 'Wb': Wb, 'bb': bb}
    _L1_gnn_all = _L1_gnn_setup()
    _L1_gnn_in = {k: v for k, v in _L1_gnn_all.items() if k in ('W_sa', 'a_sa', 'W_gcnb', 'b_gcnb', 'Wa', 'ba', 'Wb', 'bb')}
    del _L1_gnn_all
    return {'x': x, 'adj': adj, 'L0_gnn_W': _L0_gnn_in['W'], 'L0_gnn_b': _L0_gnn_in['b'], 'L1_gnn_W_sa': _L1_gnn_in['W_sa'], 'L1_gnn_a_sa': _L1_gnn_in['a_sa'], 'L1_gnn_W_gcnb': _L1_gnn_in['W_gcnb'], 'L1_gnn_b_gcnb': _L1_gnn_in['b_gcnb'], 'L1_gnn_Wa': _L1_gnn_in['Wa'], 'L1_gnn_ba': _L1_gnn_in['ba'], 'L1_gnn_Wb': _L1_gnn_in['Wb'], 'L1_gnn_bb': _L1_gnn_in['bb']}

def reference(x, adj, L0_gnn_W, L0_gnn_b, L1_gnn_W_sa, L1_gnn_a_sa, L1_gnn_W_gcnb, L1_gnn_b_gcnb, L1_gnn_Wa, L1_gnn_ba, L1_gnn_Wb, L1_gnn_bb):
    import jax
    import jax.numpy as jnp

    def _L0_gnn_ref(x, adjacency, node_degree, W, b):
        import jax, jax.numpy as jnp
        import numpy as np
        N = 8192
        D_IN = 256
        D_OUT = 256
        AVG_DEG = 32.0
        n = adjacency.shape[0]
        a_hat = adjacency + jnp.eye(n, dtype=adjacency.dtype)
        dinv = jax.lax.rsqrt(node_degree)
        a_norm = dinv * a_hat * dinv
        pooled = a_norm @ x + x
        return jax.nn.relu(pooled @ W + b)

    def _L1_gnn_ref(x, adj_a, adj_b, W_sa, a_sa, W_gcnb, b_gcnb, Wa, ba, Wb, bb):
        import jax, jax.numpy as jnp
        import numpy as np
        N = 3072
        D_IN = 256
        D_OUT = 256
        DENSITY = 0.005
        type_sum_a = adj_a @ x
        type_sum_b = adj_b @ x
        attn_a = jax.nn.sigmoid(jnp.concatenate([type_sum_a, x], axis=1) @ Wa.T + ba)
        attn_b = jax.nn.sigmoid(jnp.concatenate([type_sum_b, x], axis=1) @ Wb.T + bb)
        h = x @ W_sa
        Hd = h.shape[1]
        s_left = h @ a_sa[0, :Hd]
        s_right = h @ a_sa[0, Hd:]
        scores = s_left[:, None] + s_right[None, :]
        e = jnp.where(adj_a != 0, jnp.exp(-jax.nn.leaky_relu(scores, 0.01)), 0.0)
        attn = e / (jnp.sum(e, axis=1, keepdims=True) + 1e-05)
        x_a = attn @ h
        x_b = adj_b @ (x @ W_gcnb) + b_gcnb
        return jax.nn.sigmoid(attn_a * x_a + attn_b * x_b)
    deg = jnp.maximum((adj != 0).astype(jnp.float32).sum(-1), 1.0)
    x = _layernorm(x + _L0_gnn_ref(x, adj, deg[..., None], L0_gnn_W, L0_gnn_b), axis=-1)
    x = _layernorm(x + _L1_gnn_ref(x, adj, adj, L1_gnn_W_sa, L1_gnn_a_sa, L1_gnn_W_gcnb, L1_gnn_b_gcnb, L1_gnn_Wa, L1_gnn_ba, L1_gnn_Wb, L1_gnn_bb), axis=-1)
    return x

_drawn_inputs = setup_inputs


def setup_inputs(seed=0):
    import zlib

    import numpy as np

    out = dict(_drawn_inputs(seed))
    spreads = {}
    factors = {'L0_gnn_b': 8.0, 'L1_gnn_a_sa': 2.972, 'L1_gnn_b_gcnb': 8.0}
    for name, (base, spread) in spreads.items():
        noise = np.random.default_rng([zlib.crc32(name.encode()), seed]).standard_normal(out[name].shape)
        drawn = base * np.exp(spread * noise) if base else spread * noise
        out[name] = jnp.asarray(drawn.astype(out[name].dtype))
    for name, factor in factors.items():
        out[name] = (out[name] * factor).astype(out[name].dtype)
    return out
```

```python
from contextlib import ExitStack

import concourse.bass as bass
from concourse import mybir

ALU = mybir.AluOpType
ACT = mybir.ActivationFunctionType
F32 = mybir.dt.float32
F32R = mybir.dt.float32r
BF16 = mybir.dt.bfloat16
U8 = mybir.dt.uint8

P = 128
CHUNK = 512
TPB = CHUNK // P
EPS_NORM = 1e-5
EPS_SUM = 1e-5
SLOPE = 0.01
RAW_SLOTS = 4
XS_SLOTS = 4
EM_SLOTS = 4
EH_SLOTS = 4
AF_SLOTS = 4
EPI_FROM = 4
EPI_EVERY = 3
PEELED = 20


def two_layer_graph_kernel(nc, x, adj, W0, b0, Wsa, asa, Wg, bg, Wa, ba, Wb, bb, out):
    N, D = x.shape
    NT = N // P
    NB = N // CHUNK
    KC = D // P
    QB = NT // 4
    HALF = N // 2
    STEPS = NT

    x1_dram = nc.dram_tensor("x1_parts", [N, 2 * D], F32, kind="Internal").ap()
    sl_dram = nc.dram_tensor("s_left", [N, 1], F32, kind="Internal").ap()

    with ExitStack() as ctx:
        place = [(nc.sbuf_base + 31) // 32 * 32]

        def sb(name, shape, dt, at=None):
            size = 1
            for n in shape[1:]:
                size *= n
            size = (size * mybir.dt.size(dt) + 31) // 32 * 32
            if at is None:
                at = place[0]
                place[0] += size
            assert at + size <= nc.sbuf_usable_end, (name, at + size - nc.sbuf_usable_end)
            return nc.alloc_sbuf_tensor_at(name, shape, dt, offset=at), at, at + size

        def keep(name, shape, dt):
            return sb(name, shape, dt)[0]

        def sem(name):
            return ctx.enter_context(nc.semaphore(name))

        adjT, _, _ = sb("adjT", [P, NB, STEPS, CHUNK], U8)
        ident_b = keep("ident_b", [P, P], BF16)
        ident_f = keep("ident_f", [P, P], F32)
        ones_f = keep("ones_f", [P, P], F32)
        degh = keep("degh", [P, NT, 2], F32)
        deg = keep("deg", [P, NT], F32)
        dinv = keep("dinv", [P, NT], F32)
        kself = keep("kself", [P, NT], F32)
        dots = keep("dots", [P, NT, 4], F32)
        nsr = keep("nsr", [P, NT], F32)
        qsr = keep("qsr", [P, NT], F32)
        esl = keep("esl", [P, NT], F32)
        epsrow = keep("epsrow", [P, NT], F32)
        gatex = keep("gatex", [P, NT, 2], F32)
        consts = keep("consts", [P, 4], F32)
        gbias = keep("gbias", [P, 2], F32)
        stats = keep("stats", [P, 2, 6], F32)
        mv = keep("mv", [P, 2, 2], F32)
        vare = keep("vare", [P, 2], F32)
        rstd = keep("rstd", [P, 2], F32)
        lg = keep("lg", [P, 2, 2], F32)
        eg = keep("eg", [P, 2, 2], F32)
        gc = keep("gc", [P, 2, 2], F32)
        gr = keep("gr", [P, 2, 2], F32)
        den_sb = keep("den_sb", [P, TPB], F32)
        Wsa_sb = keep("Wsa_sb", [P, KC, D], F32)
        Wg_sb = keep("Wg_sb", [P, KC, D + 2], F32)
        bgB = keep("bgB", [P, D], F32)
        b0B = keep("b0B", [P, D], F32)
        VB = keep("VB", [P, 4, D], F32)

        base = place[0]
        gst, _, e_g = sb("gst", [P, NT, D], F32)
        ghi, _, _ = sb("ghi", [P, NT, D], F32R, at=base)
        raw, a_raw, _ = sb("raw", [P, RAW_SLOTS, HALF], F32)
        glo, _, _ = sb("glo", [P, NT, D], F32R, at=a_raw)
        W0_sb, a_w0, _ = sb("W0_sb", [P, KC, D], F32)
        xin, _, _ = sb("xin", [P, 2, D], F32)
        x1p, _, e1 = sb("x1p", [P, 2, 2 * D], F32R, at=a_w0)
        assert e1 <= place[0]
        xT, _, _ = sb("xT", [P, 2, D], F32)
        junk, a_junk, _ = sb("junk", [P, 2, HALF], U8)
        ghs, _, e1 = sb("ghs", [P, 2, D], F32R, at=a_junk)
        u, _, e1 = sb("u", [P, 2, D], F32, at=e1)
        assert e1 <= place[0]
        af0, a_af0, _ = sb("af0", [P, 2, CHUNK], F32R)
        aB, _, e1 = sb("aB", [P, 2, D], F32, at=a_af0)
        diag, _, e1 = sb("diag", [P, 4, P], F32, at=e1)
        assert e1 <= place[0]
        xres, _, _ = sb("xres", [P, 2, D], F32)
        djunk, _, _ = sb("djunk", [P, D], F32)
        place[0] = base
        xs, _, _ = sb("xs", [P, XS_SLOTS, 2 * D], F32R)
        af, _, _ = sb("af", [P, AF_SLOTS, CHUNK], F32R)
        e1x, _, _ = sb("e1x", [P, 2, CHUNK], F32)
        em, _, _ = sb("em", [P, EM_SLOTS, CHUNK], F32)
        ehi, _, _ = sb("ehi", [P, EH_SLOTS, CHUNK], F32R)
        elo, _, _ = sb("elo", [P, EH_SLOTS, CHUNK], F32R)
        slB, _, _ = sb("slB", [P, NB, CHUNK], F32)
        acc, _, _ = sb("acc", [P, CHUNK], F32)
        otA, _, _ = sb("otA", [P, KC, CHUNK], F32)
        otE, _, _ = sb("otE", [P, KC, CHUNK], F32)
        xe, _, _ = sb("xe", [P, 2, 2 * D], F32)
        w, _, _ = sb("w", [P, 2, D], F32)
        r, _, _ = sb("r", [P, 2, D], F32)
        res, _, _ = sb("res", [P, 2, D], F32)

        bank = [ctx.enter_context(nc.psum_tensor(f"bank{i}", [P, CHUNK], F32)) for i in range(8)]
        turned = [bank[q][:, :].bitcast(BF16).rearrange("p (j i) -> p j i", j=QB) for q in range(4)]
        xT_ps, xw_ps, prep_ps = bank[4], bank[5], bank[6]
        accA, accE = bank[0:2], bank[2:4]
        qE, qA = [bank[4], bank[6]], [bank[5], bank[7]]
        den_ps = bank[4]

        s_const = sem("s_const")
        s_past = sem("s_past")
        s_w = sem("s_w")
        s_w2 = sem("s_w2")
        s_prep = sem("s_prep")
        s_prep_pe = sem("s_prep_pe")
        s_raw = [sem(f"s_raw{i}") for i in range(RAW_SLOTS)]
        s_xin = [sem(f"s_xin{i}") for i in range(2)]
        s_xT = sem("s_xT")
        s_xTc = sem("s_xTc")
        s_xw = sem("s_xw")
        s_turn = [sem(f"s_turn{q}") for q in range(4)]
        s_at = [sem(f"s_at{q}") for q in range(4)]
        s_degh = sem("s_degh")
        s_deg = sem("s_deg")
        s_dinv = sem("s_dinv")
        s_kself = sem("s_kself")
        s_gst = sem("s_gst")
        s_ghs = sem("s_ghs")
        s_glo = sem("s_glo")
        s_ghi = sem("s_ghi")
        s_af0 = sem("s_af0")
        s_l0 = sem("s_l0")
        s_free0 = sem("s_free0")
        s_c0 = sem("s_c0")
        s_rstd0 = sem("s_rstd0")
        s_xres = [sem(f"s_xres{i}") for i in range(2)]
        s_x1 = sem("s_x1")
        s_dots = sem("s_dots")
        s_x1out = [sem(f"s_x1out{i}") for i in range(2)]
        s_slout = sem("s_slout")
        s_tab = sem("s_tab")
        s_tabe = sem("s_tabe")
        s_slB = sem("s_slB")
        s_xs = [sem(f"s_xs{i}") for i in range(XS_SLOTS)]
        s_af = sem("s_af")
        s_afu = sem("s_afu")
        s_e1 = sem("s_e1")
        s_em = sem("s_em")
        s_ehi = sem("s_ehi")
        s_elo = sem("s_elo")
        s_rs = sem("s_rs")
        s_step = sem("s_step")
        s_otA = sem("s_otA")
        s_otE = sem("s_otE")
        s_denp = sem("s_denp")
        s_den = sem("s_den")
        s_q = sem("s_q")
        s_qr = sem("s_qr")
        s_lg = sem("s_lg")
        s_eg = sem("s_eg")
        s_w1 = sem("s_w1")
        s_c1 = sem("s_c1")
        s_th = sem("s_th")
        s_mv = sem("s_mv")
        s_rstd1 = sem("s_rstd1")
        s_res = sem("s_res")
        s_xe = [sem(f"s_xe{i}") for i in range(2)]
        s_out = [sem(f"s_out{i}") for i in range(2)]

        def on_all(row):
            return row.broadcast_to([P, row.shape[-1]])

        def past(eng):
            eng.sem_inc(s_past, 1)

        block = ctx.enter_context(nc.Block())

        @block.sync
        def _(sp):
            def load_tile(ib, t, first):
                nt = ib * TPB + t
                if not (first and t < 2):
                    sp.wait_ge(s_xT, nt - 1)
                past(sp)
                sp.dma_start(xin[:, t % 2, :], x[bass.ds(nt * P, P), :]).then_inc(s_xin[t % 2], 16)
                for h in range(2):
                    slot = (2 * t + h) % RAW_SLOTS
                    if not (first and t < 2):
                        sp.wait_ge(s_turn[2 * h + 1], nt - 1)
                        past(sp)
                        sp.wait_ge(s_degh, 2 * nt + h - 3)
                    past(sp)
                    sp.dma_start(raw[:, slot, :], adj[bass.ds(nt * P, P), h * HALF:(h + 1) * HALF])\
                        .then_inc(s_raw[slot], 16)

            sp.dma_start(W0_sb[:, :, :], W0.rearrange("(c p) n -> p c n", p=P)).then_inc(s_w, 16)
            sp.dma_start(Wsa_sb[:, :, :], Wsa.rearrange("(c p) n -> p c n", p=P)).then_inc(s_w, 16)
            for a in range(2):
                sp.dma_start(aB[:, a, :], on_all(asa[:, a * D:(a + 1) * D])).then_inc(s_w, 16)
            for t in range(TPB):
                load_tile(0, t, True)
            for a, v in enumerate((Wa, Wb)):
                sp.dma_start(VB[:, 2 + a, :], on_all(v[:, D:2 * D])).then_inc(s_w2, 16)
                sp.dma_start(Wg_sb[:, :, D + a:D + a + 1],
                             v[0:1, 0:D].rearrange("o (c p) -> p c o", p=P),
                             allow_slow_non_contiguous=True).then_inc(s_w2, 16)
            sp.dma_start(Wg_sb[:, :, 0:D], Wg.rearrange("(c p) n -> p c n", p=P)).then_inc(s_w2, 16)
            sp.dma_start(b0B[:, :], on_all(b0.rearrange("(o n) -> o n", o=1))).then_inc(s_w2, 16)
            sp.dma_start(bgB[:, :], on_all(bg.rearrange("(o n) -> o n", o=1))).then_inc(s_w2, 16)
            for a, v in enumerate((ba, bb)):
                sp.dma_start(gbias[:, a:a + 1], on_all(v.rearrange("(o n) -> o n", o=1)))\
                    .then_inc(s_w2, 16)
            with sp.Fori(1, NB) as ib:
                for t in range(TPB):
                    load_tile(ib, t, False)

            def res_in(ib, t, first):
                nt = ib * TPB + t
                if not (first and t < 2):
                    sp.wait_ge(s_dots, nt - 1)
                past(sp)
                sp.dma_start(xres[:, t % 2, :], x[bass.ds(nt * P, P), :]).then_inc(s_xres[t % 2], 16)

            def x1_out(ib, t):
                nt = ib * TPB + t
                sp.wait_ge(s_x1, nt + 1)
                past(sp)
                sp.dma_start(x1_dram[bass.ds(nt * P, P), :], x1p[:, t % 2, :].bitcast(F32))\
                    .then_inc(s_x1out[t % 2], 16)
                sp.wait_ge(s_dots, nt + 1)
                past(sp)
                sp.dma_start(sl_dram[bass.ds(nt * P, P), :], dots[:, bass.ds(nt, 1), 0:1]
                             .rearrange("p a b -> p (a b)")).then_inc(s_slout, 16)

            for t in range(TPB):
                if t >= 2:
                    x1_out(0, t - 2)
                res_in(0, t, True)
            with sp.Fori(1, NB) as ib:
                for t in range(TPB):
                    x1_out(ib - 1 if t < 2 else ib, (t + 2) % TPB)
                    res_in(ib, t, False)
            for t in range(2, TPB):
                x1_out(NB - 1, t)

            for i in range(2):
                sp.wait_ge(s_x1out[i], 16 * NT // 2)
            sp.wait_ge(s_slout, 16 * NT)
            sp.wait_ge(s_tabe, 2)
            sp.wait_ge(s_tab, 4)

            def xs_in(n, jt, k, first):
                if not first:
                    sp.wait_ge(s_step, n - XS_SLOTS + 1)
                past(sp)
                sp.dma_start(xs[:, k % XS_SLOTS, :].bitcast(F32), x1_dram[bass.ds(jt * P, P), :])\
                    .then_inc(s_xs[k % XS_SLOTS], 16)

            def xe_in(ibp, t, first):
                nt = ibp * TPB + t
                if not (first and t < 2):
                    sp.wait_ge(s_mv, nt - 1)
                past(sp)
                sp.dma_start(xe[:, t % 2, :], x1_dram[bass.ds(nt * P, P), :]).then_inc(s_xe[t % 2], 16)

            def res_out(ibp, t):
                nt = ibp * TPB + t
                sp.wait_ge(s_res, nt + 1)
                past(sp)
                sp.dma_start(out[bass.ds(nt * P, P), :], res[:, t % 2, :]).then_inc(s_out[t % 2], 16)

            for k in range(XS_SLOTS):
                if k < 2:
                    sp.dma_start(slB[:, k, :], on_all(sl_dram[k * CHUNK:(k + 1) * CHUNK, :].rearrange("n o -> o n"))).then_inc(s_slB, 16)
                xs_in(k, k, k, True)
            for k in range(2, NB):
                sp.dma_start(slB[:, k, :], on_all(sl_dram[k * CHUNK:(k + 1) * CHUNK, :].rearrange("n o -> o n"))).then_inc(s_slB, 16)
            with sp.Fori(XS_SLOTS // XS_SLOTS, STEPS // XS_SLOTS) as four:
                jt = four * XS_SLOTS
                for k in range(XS_SLOTS):
                    xs_in(jt + k, jt + k, k, False)

            def block_streams(p, first):
                n0 = p * STEPS + STEPS
                for k in range(PEELED):
                    xs_in(n0 + k, k, k, False)
                    if k % EPI_EVERY == 0 and k // EPI_EVERY < TPB:
                        xe_in(p, k // EPI_EVERY, first)
                    if k >= EPI_FROM + 7 and (k - EPI_FROM - 7) % EPI_EVERY == 0 and (k - EPI_FROM - 7) // EPI_EVERY < TPB - 1:
                        res_out(p, (k - EPI_FROM - 7) // EPI_EVERY)
                with sp.Fori(PEELED // XS_SLOTS, STEPS // XS_SLOTS) as four:
                    jt = four * XS_SLOTS
                    for k in range(XS_SLOTS):
                        xs_in(n0 + jt + k, jt + k, k, False)
                res_out(p, TPB - 1)

            block_streams(0, True)
            with sp.Fori(1, NB - 1) as p:
                block_streams(p, False)
            for t in range(TPB):
                xe_in(NB - 1, t, False)
                if t > 0:
                    res_out(NB - 1, t - 1)
            res_out(NB - 1, TPB - 1)
            for i in range(2):
                sp.wait_ge(s_out[i], 16 * NT // 2)

        @block.gpsimd
        def _(pool):
            for tile in (ident_f, ident_b):
                pool.memset(tile[:, :], 0.0).then_inc(s_const, 1)
            pool.memset(ones_f[:, :], 1.0).then_inc(s_const, 1)
            for c, v in enumerate((-0.5, -1.0, EPS_NORM)):
                pool.memset(consts[:, c:c + 1], v).then_inc(s_const, 1)
            pool.wait_ge(s_const, 6)
            for tile in (ident_f, ident_b):
                pool.affine_select(out=tile[:, :], in_=tile[:, :], compare_op=ALU.not_equal, fill=1.0,
                                   base=0, pattern=[[-1, P]], channel_multiplier=1).then_inc(s_const, 1)
            with pool.Fori(0, NT) as nt:
                pool.wait_ge(s_deg, nt + 1)
                pool.tensor_tensor(dinv[:, bass.ds(nt, 1)], deg[:, bass.ds(nt, 1)], consts[:, 1:2], ALU.pow)\
                    .then_inc(s_dinv, 1)
            pool.wait_ge(s_dinv, NT)
            pool.tensor_tensor(kself[:, :], ones_f[:, 0:NT], dinv[:, :], ALU.add).then_inc(s_kself, 1)

            def norm_scale(i, seen, done, count):
                pool.wait_ge(seen, count + 1)
                pool.tensor_tensor(vare[:, i:i + 1], mv[:, i, 1:2], consts[:, 2:3], ALU.add).then_inc(done, 1)
                pool.wait_ge(done, 2 * count + 1)
                pool.tensor_tensor(rstd[:, i:i + 1], vare[:, i:i + 1], consts[:, 0:1], ALU.pow).then_inc(done, 1)

            with pool.Fori(0, NT // 2) as pair:
                nt = pair * 2
                for i in range(2):
                    pool.wait_ge(s_c0, TILE0 * (nt + i) + AGGR0)
                    pool.tensor_tensor(vare[:, i:i + 1], mv[:, i, 1:2], consts[:, 2:3], ALU.add)\
                        .then_inc(s_rstd0, 1)
                    pool.wait_ge(s_rstd0, 2 * (nt + i) + 1)
                    pool.tensor_tensor(rstd[:, i:i + 1], vare[:, i:i + 1], consts[:, 0:1], ALU.pow)\
                        .then_inc(s_rstd0, 1)

            def sum_first(n, ib_first, p):
                if not ib_first:
                    pool.wait_ge(s_denp, p + 1)
                pool.wait_ge(s_em, n + 1)
                if not ib_first:
                    pool.wait_ge(s_rs, n)
                past(pool)
                pool.tensor_copy(acc[:, :], em[:, 0, :]).then_inc(s_rs, 1)

            def sum_step(n, k):
                pool.wait_ge(s_em, n + 1)
                pool.wait_ge(s_rs, n)
                pool.tensor_tensor(acc[:, :], acc[:, :], em[:, k % EM_SLOTS, :], ALU.add).then_inc(s_rs, 1)

            sum_first(0, True, None)
            for k in range(1, EM_SLOTS):
                sum_step(k, k)
            with pool.Fori(EM_SLOTS // EM_SLOTS, STEPS // EM_SLOTS) as four:
                jt = four * EM_SLOTS
                for k in range(EM_SLOTS):
                    sum_step(jt + k, k)
            with pool.Fori(0, NB - 1) as p:
                n0 = p * STEPS + STEPS
                for k in range(PEELED):
                    if k == 0:
                        sum_first(n0, False, p)
                    else:
                        sum_step(n0 + k, k)
                    if k >= EPI_FROM + 3 and (k - EPI_FROM - 3) % EPI_EVERY == 0 and (k - EPI_FROM - 3) // EPI_EVERY < TPB:
                        t = (k - EPI_FROM - 3) // EPI_EVERY
                        norm_scale(t % 2, s_mv, s_rstd1, p * TPB + t)
                with pool.Fori(PEELED // EM_SLOTS, STEPS // EM_SLOTS) as four:
                    jt = four * EM_SLOTS
                    for k in range(EM_SLOTS):
                        sum_step(n0 + jt + k, k)
            for t in range(TPB):
                norm_scale(t % 2, s_mv, s_rstd1, (NB - 1) * TPB + t)

        @block.scalar
        def _(act):
            def load_tile(ib, t, first):
                nt = ib * TPB + t
                for h in range(2):
                    slot = (2 * t + h) % RAW_SLOTS
                    act.wait_ge(s_raw[slot], 32 * ib + 16 * (t // 2) + 16)
                    if not (first and t == 0):
                        act.wait_ge(s_degh, 2 * nt + h - 1)
                    past(act)
                    act.activation(junk[:, h, :], raw[:, slot, :], ACT.Copy,
                                   accum_out=degh[:, bass.ds(nt, 1), h:h + 1]).then_inc(s_degh, 1)
                    if h == 0:
                        act.wait_ge(s_xT, nt + 1)
                        if not (first and t < 2):
                            act.wait_ge(s_xw, nt - 1)
                        act.copy(xT[:, t % 2, :], xT_ps[:, 0:D]).then_inc(s_xTc, 1)
                act.wait_ge(s_turn[3], nt + 1)
                act.copy(adjT[:, bass.ds(ib, 1), 3 * QB:4 * QB, t * P:(t + 1) * P]
                         .rearrange("p a j i -> p (a j) i"), turned[3]).then_inc(s_at[3], 1)

            for t in range(TPB):
                load_tile(0, t, True)
            with act.Fori(1, NB) as ib:
                for t in range(TPB):
                    load_tile(ib, t, False)

            def g_high(jt):
                act.wait_ge(s_glo, jt + 1)
                act.copy(ghi[:, bass.ds(jt, 1), :], gst[:, bass.ds(jt, 1), :]).then_inc(s_ghi, 1)

            def chunk0(n, ib, jt, k, first):
                if not first:
                    act.wait_ge(s_l0, n - 1)
                act.copy(af0[:, k, :], adjT[:, bass.ds(ib, 1), bass.ds(jt, 1), :]
                         .rearrange("p a b i -> p (a b i)")).then_inc(s_af0, 1)

            act.wait_ge(s_gst, NT)
            for q in range(4):
                act.wait_ge(s_at[q], NT)
            for k in range(2):
                g_high(k)
                chunk0(k, 0, k, k, True)
            with act.Fori(2 // 2, STEPS // 2) as pair:
                jt = pair * 2
                for k in range(2):
                    g_high(jt + k)
                    chunk0(jt + k, 0, jt + k, k, False)
            with act.Fori(1, NB) as ib:
                with act.Fori(0, STEPS // 2) as pair:
                    jt = pair * 2
                    for k in range(2):
                        chunk0(ib * STEPS + jt + k, ib, jt + k, k, False)

            act.wait_ge(s_dots, NT)
            act.activation(qsr[:, :], dots[:, :, 1], ACT.Exp, scale=-SLOPE).then_inc(s_tabe, 1)
            act.activation(esl[:, :], dots[:, :, 0], ACT.Exp, scale=SLOPE).then_inc(s_tabe, 1)
            act.wait_ge(s_tab, 1)
            act.wait_ge(s_l0, NB * STEPS)
            for i in range(2):
                act.wait_ge(s_x1out[i], 16 * NT // 2)

            def step(n, ib, jt, k, first, last_high=True):
                if not first:
                    act.wait_ge(s_afu, n - AF_SLOTS + 1)
                chunk = adjT[:, bass.ds(ib, 1), bass.ds(jt, 1), :].rearrange("p a b i -> p (a b i)")
                act.copy(af[:, k % AF_SLOTS, :], chunk).then_inc(s_af, 1)
                act.activation(e1x[:, k % 2, :], slB[:, bass.ds(ib, 1), :].rearrange("p a i -> p (a i)"),
                               ACT.Exp, bias=nsr[:, bass.ds(jt, 1)], scale=SLOPE - 1.0).then_inc(s_e1, 1)
                if last_high:
                    high(n, k, first)

            def high(n, k, first):
                act.wait_ge(s_em, n)
                if not first:
                    act.wait_ge(s_step, n - EH_SLOTS + 1)
                act.copy(ehi[:, (k - 1) % EH_SLOTS, :], em[:, (k - 1) % EM_SLOTS, :]).then_inc(s_ehi, 1)

            act.wait_ge(s_slB, 16 * NB)
            for k in range(4):
                step(k, 0, k, k, True, last_high=k > 0)
            with act.Fori(4 // 4, STEPS // 4) as four:
                jt = four * 4
                for k in range(4):
                    step(jt + k, 0, jt + k, k, False)

            def copy_A(count):
                for c in range(KC):
                    if c == 0:
                        act.wait_ge(s_step, (count + 1) * STEPS)
                        if not isinstance(count, int) or count > 0:
                            act.wait_ge(s_q, count * TPB)
                    act.copy(otA[:, c, :], accA[c][:, :]).then_inc(s_otA, 1)

            def gates(nt, i):
                act.wait_ge(s_lg, nt + 1)
                act.activation(eg[:, i, :], lg[:, i, :], ACT.Exp, scale=-1.0).then_inc(s_eg, 1)

            def tanh(nt, i):
                act.wait_ge(s_w1, nt + 1)
                act.activation(w[:, i, :], w[:, i, :], ACT.Tanh, scale=0.5).then_inc(s_th, 1)

            with act.Fori(0, NB - 1) as p:
                n0 = p * STEPS + STEPS
                for k in range(PEELED):
                    step(n0 + k, p + 1, k, k, False)
                    if k == 1:
                        copy_A(p)
                    for t in range(TPB):
                        if k == EPI_FROM + EPI_EVERY * t + 1:
                            gates(p * TPB + t, t % 2)
                        if k == EPI_FROM + EPI_EVERY * t + 2:
                            tanh(p * TPB + t, t % 2)
                with act.Fori(PEELED // 4, STEPS // 4) as four:
                    jt = four * 4
                    for k in range(4):
                        step(n0 + jt + k, p + 1, jt + k, k, False)
            high(NB * STEPS, 0, False)
            copy_A(NB - 1)
            for t in range(TPB):
                gates((NB - 1) * TPB + t, t % 2)
                tanh((NB - 1) * TPB + t, t % 2)

        @block.vector
        def _(dve):
            dve.wait_ge(s_w, 64)
            for a in range(2):
                for c in range(KC):
                    if a + c > 0:
                        dve.wait_ge(s_prep, 2 * a + c)
                    dve.scalar_tensor_tensor(out=djunk[:, :], in0=Wsa_sb[:, c, :], scalar=1.0,
                                             in1=aB[:, a, :], op0=ALU.mult, op1=ALU.mult,
                                             accum_out=lg[:, a, c:c + 1]).then_inc(s_prep, 1)
            dve.wait_ge(s_prep, 4)
            dve.wait_ge(s_const, 8)
            for a in range(2):
                for c in range(KC):
                    dve.tensor_scalar(diag[:, 2 * a + c, :], ident_f[:, :], lg[:, a, c:c + 1], None, ALU.mult)\
                        .then_inc(s_prep, 1)
            dve.wait_ge(s_prep_pe, 1)
            dve.tensor_copy(VB[:, 0:2, :], prep_ps[:, :].rearrange("p (a n) -> p a n", a=2)).then_inc(s_prep, 1)

            def load_tile(ib, t, first):
                nt = ib * TPB + t
                for q in range(3):
                    dve.wait_ge(s_turn[q], nt + 1)
                    dve.tensor_copy(adjT[:, bass.ds(ib, 1), q * QB:(q + 1) * QB, t * P:(t + 1) * P]
                                    .rearrange("p a j i -> p (a j) i"), turned[q]).then_inc(s_at[q], 1)
                dve.wait_ge(s_degh, 2 * nt + 2)
                dve.tensor_scalar(deg[:, bass.ds(nt, 1)], degh[:, bass.ds(nt, 1), 0:1].rearrange("p a b -> p (a b)"),
                                  degh[:, bass.ds(nt, 1), 1:2].rearrange("p a b -> p (a b)"), 1.0,
                                  ALU.add, ALU.max).then_inc(s_deg, 1)
                dve.wait_ge(s_xw, nt + 1)
                dve.tensor_copy(gst[:, bass.ds(nt, 1), :].rearrange("p a n -> p (a n)"), xw_ps[:, 0:D]).then_inc(s_gst, 1)

            for t in range(TPB):
                load_tile(0, t, True)
            with dve.Fori(1, NB) as ib:
                for t in range(TPB):
                    load_tile(ib, t, False)

            dve.wait_ge(s_gst, NT)
            dve.wait_ge(s_turn[3], NT)

            def g_parts(jt, k, first):
                if not first:
                    dve.wait_ge(s_glo, jt - 1)
                dve.tensor_copy(ghs[:, k:k + 1, :], gst[:, bass.ds(jt, 1), :]).then_inc(s_ghs, 1)
                dve.wait_ge(s_ghs, jt + 1)
                dve.tensor_tensor(glo[:, bass.ds(jt, 1), :], gst[:, bass.ds(jt, 1), :],
                                  ghs[:, k:k + 1, :].bitcast(F32), ALU.subtract).then_inc(s_glo, 1)

            for k in range(2):
                g_parts(k, k, True)
            with dve.Fori(2 // 2, NT // 2) as pair:
                jt = pair * 2
                for k in range(2):
                    g_parts(jt + k, k, False)
            dve.wait_ge(s_w2, 16 * 9)
            dve.wait_ge(s_kself, 1)
            dve.wait_ge(s_dinv, NT)
            dve.wait_ge(s_ghi, NT)
            dve.wait_ge(s_glo, NT)
            dve.wait_ge(s_prep, 9)

            def finish0(ib, b, t, first):
                nt = ib * TPB + t
                ui, di, ki = u[:, t % 2, :], dinv[:, bass.ds(nt, 1)], kself[:, bass.ds(nt, 1)]
                c = [nt * TILE0]

                def link(ins):
                    ins.then_inc(s_c0, 1)
                    c[0] = c[0] + 1
                    dve.wait_ge(s_c0, c[0])

                if not (first and t < 2):
                    dve.wait_ge(s_x1, nt - 1)
                    dve.wait_ge(s_dots, nt - 1)
                dve.wait_ge(s_l0, ib * STEPS + STEPS)
                link(dve.tensor_scalar(ui, bank[b][:, D:2 * D], di, None, ALU.mult))
                dve.scalar_tensor_tensor(out=ui, in0=bank[b][:, 0:D], scalar=di, in1=ui, op0=ALU.mult,
                                         op1=ALU.add).then_inc(s_free0, 1)
                dve.wait_ge(s_free0, nt + 1)
                for part in (ghi, glo):
                    link(dve.scalar_tensor_tensor(
                        out=ui, in0=part[:, bass.ds(nt, 1), :].rearrange("p a n -> p (a n)").bitcast(F32),
                        scalar=ki, in1=ui, op0=ALU.mult, op1=ALU.add))
                link(dve.tensor_tensor(ui, ui, b0B[:, :], ALU.add))
                dve.wait_ge(s_xres[t % 2], 32 * ib + 16 * (t // 2) + 16)
                link(dve.scalar_tensor_tensor(out=ui, in0=ui, scalar=0.0, in1=xres[:, t % 2, :],
                                              op0=ALU.max, op1=ALU.add))
                link(dve.bn_stats(stats[:, t % 2, :], ui))
                past(dve)
                link(dve.bn_aggr(mv[:, t % 2, :], stats[:, t % 2, :]))
                dve.wait_ge(s_rstd0, 2 * nt + 2)
                link(dve.tensor_scalar(ui, ui, mv[:, t % 2, 0:1], rstd[:, t % 2:t % 2 + 1], ALU.subtract, ALU.mult))
                if not (first and t < 2):
                    dve.wait_ge(s_x1out[t % 2], 32 * ib + 16 * (t // 2))
                link(dve.tensor_copy(x1p[:, t % 2, 0:D], ui))
                dve.tensor_tensor(x1p[:, t % 2, D:2 * D], ui, x1p[:, t % 2, 0:D].bitcast(F32), ALU.subtract)\
                    .then_inc(s_x1, 1)
                if not (first and t == 0):
                    dve.wait_ge(s_dots, nt)
                for v in range(4):
                    ins = dve.scalar_tensor_tensor(
                        out=djunk[:, :], in0=ui, scalar=1.0, in1=VB[:, v, :], op0=ALU.mult, op1=ALU.mult,
                        accum_out=dots[:, bass.ds(nt, 1), v:v + 1].rearrange("p a b -> p (a b)"))
                    if v < 3:
                        link(ins)
                ins.then_inc(s_dots, 1)

            for ib in range(2):
                for t in range(TPB):
                    finish0(ib, (ib % 2) * TPB + t, t, ib == 0)
            with dve.Fori(2 // 2, NB // 2) as pair:
                ib2 = pair * 2
                for par in range(2):
                    for t in range(TPB):
                        finish0(ib2 + par, par * TPB + t, t, False)

            dve.wait_ge(s_dots, NT)
            dve.tensor_scalar(nsr[:, :], dots[:, :, 1], -1.0, None, ALU.mult).then_inc(s_tab, 1)
            for a in range(2):
                dve.tensor_scalar(gatex[:, :, a], dots[:, :, 2 + a], gbias[:, a:a + 1], None, ALU.add)\
                    .then_inc(s_tab, 1)
            dve.wait_ge(s_tabe, 2)
            dve.tensor_scalar(epsrow[:, :], esl[:, :], EPS_SUM, None, ALU.mult).then_inc(s_tab, 1)
            dve.wait_ge(s_tab, 4)
            for i in range(2):
                dve.wait_ge(s_x1out[i], 16 * NT // 2)

            def step(n, ib, jt, k, first):
                dve.wait_ge(s_e1, n + 1)
                if not first:
                    dve.wait_ge(s_elo, n - EM_SLOTS + 1)
                    dve.wait_ge(s_rs, n - EM_SLOTS + 1)
                chunk = adjT[:, bass.ds(ib, 1), bass.ds(jt, 1), :].rearrange("p a b i -> p (a b i)")
                dve.scalar_tensor_tensor(out=em[:, k % EM_SLOTS, :], in0=e1x[:, k % 2, :],
                                         scalar=qsr[:, bass.ds(jt, 1)], in1=chunk,
                                         op0=ALU.min, op1=ALU.mult).then_inc(s_em, 1)
                if not (first and k == 0):
                    low(n, k, first)

            def low(n, k, first):
                dve.wait_ge(s_ehi, n)
                if not first:
                    dve.wait_ge(s_step, n - EH_SLOTS + 1)
                dve.tensor_tensor(elo[:, (k - 1) % EH_SLOTS, :], em[:, (k - 1) % EM_SLOTS, :],
                                  ehi[:, (k - 1) % EH_SLOTS, :].bitcast(F32), ALU.subtract).then_inc(s_elo, 1)

            def copy_E(count):
                dve.wait_ge(s_step, (count + 1) * STEPS)
                if not isinstance(count, int) or count > 0:
                    dve.wait_ge(s_q, count * TPB)
                for c in range(KC):
                    dve.tensor_copy(otE[:, c, :], accE[c][:, :]).then_inc(s_otE, 1)

            def sums(count):
                dve.wait_ge(s_denp, count + 1)
                if not isinstance(count, int) or count > 0:
                    dve.wait_ge(s_w1, count * TPB)
                dve.tensor_tensor(den_sb[:, :], den_ps[:, D + 4:D + 4 + TPB],
                                  epsrow[:, bass.ds(count * TPB, TPB)], ALU.add).then_inc(s_den, 1)

            def logits(nt, i):
                dve.wait_ge(s_q, nt + 1)
                dve.tensor_tensor(lg[:, i, :], qA[i][:, D:D + 2],
                                  gatex[:, bass.ds(nt, 1), :].rearrange("p a b -> p (a b)"), ALU.add)\
                    .then_inc(s_lg, 1)

            def gated_sum(p, nt, t):
                i, c = t % 2, [nt * TILE1]

                def link(ins):
                    ins.then_inc(s_c1, 1)
                    c[0] = c[0] + 1
                    dve.wait_ge(s_c1, c[0])

                dve.wait_ge(s_eg, nt + 1)
                dve.wait_ge(s_den, p + 1)
                link(dve.tensor_scalar(gc[:, i, :], eg[:, i, :], 1.0, None, ALU.add))
                link(dve.tensor_tensor(gc[:, i, 0:1], gc[:, i, 0:1], den_sb[:, t:t + 1], ALU.mult))
                link(dve.reciprocal(gr[:, i, :], gc[:, i, :]))
                link(dve.tensor_scalar(w[:, i, :], qE[i][:, 0:D], gr[:, i, 0:1], None, ALU.mult))
                dve.scalar_tensor_tensor(out=w[:, i, :], in0=qA[i][:, 0:D], scalar=gr[:, i, 1:2],
                                         in1=w[:, i, :], op0=ALU.mult, op1=ALU.add).then_inc(s_qr, 1)
                dve.wait_ge(s_qr, nt + 1)
                dve.scalar_tensor_tensor(out=w[:, i, :], in0=bgB[:, :], scalar=gr[:, i, 1:2],
                                         in1=w[:, i, :], op0=ALU.mult, op1=ALU.add).then_inc(s_w1, 1)

            def residual(p, nt, t):
                i, c = t % 2, [nt * TILE1 + 4]

                def link(ins):
                    ins.then_inc(s_c1, 1)
                    c[0] = c[0] + 1
                    dve.wait_ge(s_c1, c[0])

                dve.wait_ge(s_th, nt + 1)
                dve.wait_ge(s_xe[i], 32 * p + 16 * (t // 2) + 16)
                link(dve.scalar_tensor_tensor(out=r[:, i, :], in0=w[:, i, :], scalar=0.5, in1=xe[:, i, 0:D],
                                              op0=ALU.mult, op1=ALU.add))
                link(dve.scalar_tensor_tensor(out=r[:, i, :], in0=xe[:, i, D:2 * D], scalar=0.5, in1=r[:, i, :],
                                              op0=ALU.add, op1=ALU.add))
                link(dve.bn_stats(stats[:, i, :], r[:, i, :]))
                past(dve)
                dve.bn_aggr(mv[:, i, :], stats[:, i, :]).then_inc(s_mv, 1)

            def normalise(p, nt, t, first):
                i = t % 2
                dve.wait_ge(s_rstd1, 2 * nt + 2)
                if not (first and t < 2):
                    dve.wait_ge(s_out[i], 32 * p + 16 * (t // 2))
                dve.tensor_scalar(res[:, i, :], r[:, i, :], mv[:, i, 0:1], rstd[:, i:i + 1],
                                  ALU.subtract, ALU.mult).then_inc(s_res, 1)

            for k in range(4):
                step(k, 0, k, k, True)
            with dve.Fori(4 // 4, STEPS // 4) as four:
                jt = four * 4
                for k in range(4):
                    step(jt + k, 0, jt + k, k, False)

            def block_steps(p, first):
                n0 = p * STEPS + STEPS
                for k in range(PEELED):
                    step(n0 + k, p + 1, k, k, False)
                    if k == 1:
                        copy_E(p)
                    if k == 3:
                        sums(p)
                    for t in range(TPB):
                        nt, s = p * TPB + t, EPI_FROM + EPI_EVERY * t
                        if k == s:
                            logits(nt, t % 2)
                        if k == s + 1:
                            gated_sum(p, nt, t)
                        if k == s + 3:
                            residual(p, nt, t)
                        if k == s + 5:
                            normalise(p, nt, t, first)
                with dve.Fori(PEELED // 4, STEPS // 4) as four:
                    jt = four * 4
                    for k in range(4):
                        step(n0 + jt + k, p + 1, jt + k, k, False)

            block_steps(0, True)
            with dve.Fori(1, NB - 1) as p:
                block_steps(p, False)
            low(NB * STEPS, 0, False)
            copy_E(NB - 1)
            sums(NB - 1)
            for t in range(TPB):
                nt = (NB - 1) * TPB + t
                logits(nt, t % 2)
                gated_sum(NB - 1, nt, t)
                residual(NB - 1, nt, t)
                normalise(NB - 1, nt, t, False)

        @block.tensor
        def _(pe):
            pe.wait_ge(s_const, 8)
            pe.wait_ge(s_prep, 8)
            for v in range(4):
                ins = pe.matmul(prep_ps[:, v * P:(v + 1) * P], ones_f[:, :], diag[:, v, :], start=True, stop=True)
            ins.then_inc(s_prep_pe, 1)

            def load_tile(ib, t, first):
                nt = ib * TPB + t
                pe.wait_ge(s_xin[t % 2], 32 * ib + 16 * (t // 2) + 16)
                if not (first and t == 0):
                    pe.wait_ge(s_xTc, nt)
                for c in range(KC):
                    ins = pe.transpose(xT_ps[:, c * P:(c + 1) * P], xin[:, t % 2, c * P:(c + 1) * P], ident_f[:, :])
                ins.then_inc(s_xT, 1)
                for h in range(2):
                    slot = (2 * t + h) % RAW_SLOTS
                    bits = raw[:, slot, :].bitcast(BF16).rearrange("p (n two) -> p n two", two=2)
                    pe.wait_ge(s_raw[slot], 32 * ib + 16 * (t // 2) + 16)
                    for q in (2 * h, 2 * h + 1):
                        if not (first and t == 0):
                            pe.wait_ge(s_at[q], nt)
                        for j in range(QB):
                            col = ((q % 2) * QB + j) * P
                            ins = pe.transpose(turned[q][:, j, :], bits[:, col:col + P, 1], ident_b[:, :])
                        ins.then_inc(s_turn[q], 1)
                    if h == 0:
                        pe.wait_ge(s_xTc, nt + 1)
                        if not (first and t == 0):
                            pe.wait_ge(s_gst, nt)
                        for c in range(KC):
                            ins = pe.matmul(xw_ps[:, 0:D], xT[:, t % 2, c * P:(c + 1) * P], W0_sb[:, c, :],
                                            start=(c == 0), stop=(c == KC - 1))
                        ins.then_inc(s_xw, 1)

            for t in range(TPB):
                load_tile(0, t, True)
            with pe.Fori(1, NB) as ib:
                for t in range(TPB):
                    load_tile(ib, t, False)

            def step0(n, par, jt, k, start, stop, parts):
                pe.wait_ge(s_af0, n + 1)
                if parts:
                    pe.wait_ge(s_ghi, jt + 1)
                    pe.wait_ge(s_glo, jt + 1)
                for t in range(TPB):
                    b = bank[par * TPB + t][:, :]
                    for c, part in enumerate((ghi, glo)):
                        ins = pe.matmul(b[:, c * D:(c + 1) * D], af0[:, k, t * P:(t + 1) * P],
                                        part[:, bass.ds(jt, 1), :].rearrange("p a n -> p (a n)"),
                                        start=start and c == 0, stop=stop, skip_group_check=True)
                ins.then_inc(s_l0, 1)

            def block0(ib, par, parts, wait):
                if wait:
                    pe.wait_ge(s_free0, ib * TPB - TPB)
                n0 = ib * STEPS
                for k in range(2):
                    step0(n0 + k, par, k, k, k == 0, False, parts)
                with pe.Fori(2 // 2, (STEPS - 2) // 2) as pair:
                    jt = pair * 2
                    for k in range(2):
                        step0(n0 + jt + k, par, jt + k, k, False, False, parts)
                for k in range(2):
                    step0(n0 + STEPS - 2 + k, par, STEPS - 2 + k, k, False, k == 1, parts)

            pe.wait_ge(s_gst, NT)
            pe.wait_ge(s_at[3], NT)
            pe.wait_ge(s_prep, 9)
            block0(0, 0, True, False)
            block0(1, 1, False, False)
            with pe.Fori(2 // 2, NB // 2) as pair:
                ib2 = pair * 2
                for par in range(2):
                    block0(ib2 + par, par, False, True)

            def step(n, k, landed, start, stop, first, p):
                tile = xs[:, k % XS_SLOTS, :]
                hi = [tile[:, c * P:(c + 1) * P] for c in range(KC)]
                lo = [tile[:, D + c * P:D + (c + 1) * P] for c in range(KC)]
                pe.wait_ge(s_xs[k % XS_SLOTS], landed)
                pe.wait_ge(s_af, n + 1)
                a, eh, el = af[:, k % AF_SLOTS, :], ehi[:, k % EH_SLOTS, :], elo[:, k % EH_SLOTS, :]
                for c in range(KC):
                    if start and not first:
                        pe.wait_ge(s_otA, KC * p + c + 1)
                    pe.matmul(accA[c][:, :], hi[c], a, start=start, stop=False, skip_group_check=True)
                    ins = pe.matmul(accA[c][:, :], lo[c], a, start=False, stop=stop, skip_group_check=True)
                ins.then_inc(s_afu, 1)
                pe.wait_ge(s_ehi, n + 1)
                for c in range(KC):
                    if start and not first:
                        pe.wait_ge(s_otE, KC * p + c + 1)
                    pe.matmul(accE[c][:, :], hi[c], eh, start=start, stop=False, skip_group_check=True)
                    pe.matmul(accE[c][:, :], lo[c], eh, start=False, stop=False, skip_group_check=True)
                pe.wait_ge(s_elo, n + 1)
                for c in range(KC):
                    ins = pe.matmul(accE[c][:, :], hi[c], el, start=False, stop=stop, skip_group_check=True)
                ins.then_inc(s_step, 1)

            def row_sums(count):
                pe.wait_ge(s_rs, (count + 1) * STEPS)
                if isinstance(count, int) and count == 0:
                    pe.wait_ge(s_free0, NB * TPB)
                else:
                    pe.wait_ge(s_qr, count * TPB)
                for t in range(TPB):
                    ins = pe.matmul(den_ps[:, D + 4 + t:D + 5 + t], acc[:, t * P:(t + 1) * P], ones_f[:, 0:1],
                                    start=True, stop=True, skip_group_check=True)
                ins.then_inc(s_denp, 1)

            def weights(p, nt, t, first):
                i = t % 2
                if t == 0:
                    pe.wait_ge(s_otA, KC * p + KC)
                    pe.wait_ge(s_otE, KC * p + KC)
                    pe.wait_ge(s_den, p + 1)
                if not (first and t < 2):
                    pe.wait_ge(s_qr, nt - 1)
                for c in range(KC):
                    pe.matmul(qE[i][:, 0:D], otE[:, c, t * P:(t + 1) * P], Wsa_sb[:, c, :],
                              start=(c == 0), stop=(c == KC - 1), skip_group_check=True)
                for c in range(KC):
                    ins = pe.matmul(qA[i][:, 0:D + 2], otA[:, c, t * P:(t + 1) * P], Wg_sb[:, c, :],
                                    start=(c == 0), stop=(c == KC - 1), skip_group_check=True)
                ins.then_inc(s_q, 1)

            per = 16 * STEPS // XS_SLOTS
            pe.wait_ge(s_free0, NB * TPB)
            for k in range(4):
                step(k, k, 16, k == 0, False, True, None)
            with pe.Fori(4 // 4, (STEPS - 4) // 4) as four:
                jt = four * 4
                for k in range(4):
                    step(jt + k, k, 4 * jt + 16, False, False, True, None)
            for k in range(4):
                step(STEPS - 4 + k, k, per, False, k == 3, True, None)

            def block_steps(p, first):
                n0, c0 = p * STEPS + STEPS, p * per + per
                for k in range(PEELED):
                    step(n0 + k, k, c0 + 16 * (k // 4) + 16, k == 0, False, False, p)
                    if k == 1:
                        row_sums(p)
                    for t in range(TPB):
                        if k == EPI_FROM + EPI_EVERY * t - 1:
                            weights(p, p * TPB + t, t, first)
                with pe.Fori(PEELED // 4, (STEPS - 4) // 4) as four:
                    jt = four * 4
                    for k in range(4):
                        step(n0 + jt + k, k, c0 + 4 * jt + 16, False, False, False, p)
                for k in range(4):
                    step(n0 + STEPS - 4 + k, k, c0 + per, False, k == 3, False, p)

            block_steps(0, True)
            with pe.Fori(1, NB - 1) as p:
                block_steps(p, False)
            row_sums(NB - 1)
            for t in range(TPB):
                weights(NB - 1, (NB - 1) * TPB + t, t, False)


TILE0 = 12
AGGR0 = 7
TILE1 = 7


_INS = ['x', 'adj', 'L0_gnn_W', 'L0_gnn_b', 'L1_gnn_W_sa', 'L1_gnn_a_sa', 'L1_gnn_W_gcnb', 'L1_gnn_b_gcnb',
        'L1_gnn_Wa', 'L1_gnn_ba', 'L1_gnn_Wb', 'L1_gnn_bb']
_OUTS = [((4096, 256), 'float32')]


def kernel(**inputs):
    import numpy as _np
    import concourse.bacc as _bacc
    from concourse import mybir as _mybir
    from concourse.bass_utils import run_bass_kernel_spmd as _run

    nc = _bacc.Bacc("TRN2", target_bir_lowering=False, num_devices=1, dynamic_dma_scratch_size=1024)
    arrays, args = {}, []
    for name in _INS:
        a = _np.ascontiguousarray(inputs[name])
        arrays[f"in_{name}_dram"] = a
        args.append(nc.dram_tensor(f"in_{name}_dram", a.shape, _mybir.dt.from_np(a.dtype), kind="ExternalInput").ap())
    for i, (shape, dtype) in enumerate(_OUTS):
        dt = _mybir.dt.from_np(_np.dtype(dtype))
        args.append(nc.dram_tensor(f"out_{i}_dram", shape, dt, kind="ExternalOutput").ap())
    two_layer_graph_kernel(nc, *args)
    r = _run(nc, [arrays], core_ids=[0])
    got = tuple(r.results[0][f"out_{i}_dram"] for i in range(len(_OUTS)))
    return got[0]
```

```python
from contextlib import ExitStack

import concourse.bass as bass
from concourse import mybir

ALU = mybir.AluOpType
ACT = mybir.ActivationFunctionType
F32 = mybir.dt.float32
F32R = mybir.dt.float32r
U8 = mybir.dt.uint8

P = 128
CHUNK = 512
TPB = CHUNK // P
PACK = 4
EPS_NORM = 1e-5
EPS_SUM = 1e-5
SLOPE = 0.01
ZERO = 48.0
SLOTS = 6
XS_SLOTS = 2
EM_SLOTS = 4
EH_SLOTS = 4
AF_SLOTS = 4
AHEAD = 4
LOGITS, GATES, GATED, TANH, RESIDUAL, NORMED = 5, 6, 7, 8, 9, 11
UNROLL = 8
EPI = [2, 8, 14, 20]
TILE0 = 10
AGGR0 = 5
TILE1 = 7


def two_layer_graph_kernel(nc, x, adj, W0, b0, Wsa, asa, Wg, bg, Wa, ba, Wb, bb, out):
    N, D = x.shape
    NT = N // P
    NB = N // CHUNK
    NG = NT // PACK
    KC = D // P
    QUARTER = N // 4
    SPILL = NB - SLOTS
    UNITS = 4
    JU = NT // UNITS

    x1_dram = nc.dram_tensor("x1_parts", [N, 2 * D], F32, kind="Internal").ap()
    g_dram = nc.dram_tensor("g_rows", [N, D], F32, kind="Internal").ap()
    sl_dram = nc.dram_tensor("s_left", [N, 1], F32, kind="Internal").ap()
    sr_dram = nc.dram_tensor("s_right", [N, 1], F32, kind="Internal").ap()
    spill_dram = nc.dram_tensor("adj_spill", [SPILL, P, NG * CHUNK], F32, kind="Internal").ap()

    with ExitStack() as ctx:
        place = [(nc.sbuf_base + 31) // 32 * 32]

        def sb(name, shape, dt, at=None):
            size = mybir.dt.size(dt)
            for n in shape[1:]:
                size *= n
            size = (size + 31) // 32 * 32
            if at is None:
                at = place[0]
                place[0] += size
            assert at + size <= nc.sbuf_usable_end, (name, at + size - nc.sbuf_usable_end)
            return nc.alloc_sbuf_tensor_at(name, shape, dt, offset=at), at, at + size

        def keep(name, shape, dt):
            return sb(name, shape, dt)[0]

        def sem(name):
            return ctx.enter_context(nc.semaphore(name))

        adjw = keep("adjw", [P, SLOTS, NG, CHUNK], F32)
        ident = keep("ident", [P, P], F32)
        ones = keep("ones", [P, P], F32)
        degq = keep("degq", [P, 2, 4], F32)
        degs = keep("degs", [P, 2, 4], F32)
        rdeg = keep("rdeg", [P, 4, 2], F32)
        dots = keep("dots", [P, NT, 4], F32)
        srj = keep("srj", [P, NT], F32)
        nsr = keep("nsr", [P, NT], F32)
        qsr = keep("qsr", [P, NT], F32)
        esl = keep("esl", [P, NT], F32)
        epsrow = keep("epsrow", [P, NT], F32)
        gatex = keep("gatex", [P, NT, 2], F32)
        consts = keep("consts", [P, 4], F32)
        gbias = keep("gbias", [P, 2], F32)
        stats = keep("stats", [P, 2, 6], F32)
        mv = keep("mv", [P, 2, 2], F32)
        vare = keep("vare", [P, 2], F32)
        rstd = keep("rstd", [P, 2], F32)
        lg = keep("lg", [P, 2, 2], F32)
        eg = keep("eg", [P, 2, 2], F32)
        gc = keep("gc", [P, 2, 2], F32)
        gr = keep("gr", [P, 2, 2], F32)
        den_sb = keep("den_sb", [P, TPB], F32)
        b0B = keep("b0B", [P, D], F32)
        VB = keep("VB", [P, 4, D], F32)

        base = place[0]
        G = keep("G", [P, NT, 2 * D], F32R)
        raw = keep("raw", [P, 4, QUARTER], F32)
        rowb = keep("rowb", [P, 2, N], U8)
        af0, a_af0, _ = sb("af0", [P, UNITS, JU * P], F32R)
        xj, _, at = sb("xj", [P, 2, PACK * D], F32, at=a_af0)
        gst, _, at = sb("gst", [P, 2, PACK * D], F32, at=at)
        assert at <= place[0]
        xres, a_xres, _ = sb("xres", [P, 2, D], F32)
        gres, _, _ = sb("gres", [P, 2, D], F32)
        aB, _, at = sb("aB", [P, 2, D], F32, at=a_xres)
        diag, _, at = sb("diag", [P, 4, P], F32, at=at)
        assert at <= place[0]
        u = keep("u", [P, 2, D], F32)
        x1p, a_x1p, _ = sb("x1p", [P, 2, 2 * D], F32R)
        W0_sb, _, at = sb("W0_sb", [P, KC, D], F32, at=a_x1p)
        xT, _, at = sb("xT", [P, 2, D], F32, at=at)
        assert at <= place[0]
        djunk = keep("djunk", [P, 2, D], F32)
        place[0] = base
        xs = keep("xs", [P, XS_SLOTS, PACK, 2 * D], F32R)
        af = keep("af", [P, AF_SLOTS, CHUNK], F32R)
        e1x = keep("e1x", [P, 2, CHUNK], F32)
        em = keep("em", [P, EM_SLOTS, CHUNK], F32)
        ehi = keep("ehi", [P, EH_SLOTS, CHUNK], F32R)
        elo = keep("elo", [P, EH_SLOTS, CHUNK], F32R)
        slB = keep("slB", [P, NB, CHUNK], F32)
        acc = keep("acc", [P, CHUNK], F32)
        acc_first = keep("acc_first", [P, CHUNK], F32)
        otA = keep("otA", [P, KC, CHUNK], F32)
        otE = keep("otE", [P, KC, CHUNK], F32)
        Wsa_sb = keep("Wsa_sb", [P, KC, D], F32)
        Wg_sb = keep("Wg_sb", [P, KC, D + 2], F32)
        bgB = keep("bgB", [P, D], F32)
        xe = keep("xe", [P, 2, 2 * D], F32)
        w = keep("w", [P, 2, D], F32)
        r = keep("r", [P, 2, D], F32)
        res = keep("res", [P, 2, D], F32)
        Wsa_0, _, _ = sb("Wsa_0", [P, KC, D], F32, at=base)

        bank = [ctx.enter_context(nc.psum_tensor(f"bank{i}", [P, CHUNK], F32)) for i in range(8)]
        turned = bank[2:4]
        xT_ps, xw_ps, prep_ps = bank[4:6], bank[6:8], bank[3]
        accA, accE = bank[0:2], bank[2:4]
        qE, qA = [bank[4], bank[6]], [bank[5], bank[7]]
        den_ps = bank[6]
        DEN = D + 4

        s_const = sem("s_const")
        s_past = sem("s_past")
        s_w = sem("s_w")
        s_w2 = sem("s_w2")
        s_w3 = sem("s_w3")
        s_prep = sem("s_prep")
        s_prep_pe = sem("s_prep_pe")
        s_xj = [sem(f"s_xj{i}") for i in range(2)]
        s_xT = sem("s_xT")
        s_xTc = sem("s_xTc")
        s_xw = sem("s_xw")
        s_gst = sem("s_gst")
        s_ghi = sem("s_ghi")
        s_glo = sem("s_glo")
        s_gout = [sem(f"s_gout{i}") for i in range(2)]
        s_raw = [sem(f"s_raw{i}") for i in range(4)]
        s_conv = sem("s_conv")
        s_rdeg = sem("s_rdeg")
        s_turn = sem("s_turn")
        s_word = sem("s_word")
        s_spill = sem("s_spill")
        s_af0 = sem("s_af0")
        s_mm = sem("s_mm")
        s_free0 = sem("s_free0")
        s_c0 = sem("s_c0")
        s_rstd0 = sem("s_rstd0")
        s_in = [sem(f"s_in{i}") for i in range(2)]
        s_x1 = sem("s_x1")
        s_dots = sem("s_dots")
        s_x1out = [sem(f"s_x1out{i}") for i in range(2)]
        s_slout = sem("s_slout")
        s_srj = sem("s_srj")
        s_tab = sem("s_tab")
        s_tabe = sem("s_tabe")
        s_slB = [sem(f"s_slB{i}") for i in range(2)]
        s_xs = [sem(f"s_xs{i}") for i in range(XS_SLOTS)]
        s_back = sem("s_back")
        s_af = sem("s_af")
        s_afu = sem("s_afu")
        s_e1 = sem("s_e1")
        s_em = sem("s_em")
        s_ehi = sem("s_ehi")
        s_elo = sem("s_elo")
        s_rs = sem("s_rs")
        s_step = sem("s_step")
        s_otA = sem("s_otA")
        s_otE = sem("s_otE")
        s_denp = sem("s_denp")
        s_den = sem("s_den")
        s_q = sem("s_q")
        s_qr = sem("s_qr")
        s_lg = sem("s_lg")
        s_eg = sem("s_eg")
        s_w1 = sem("s_w1")
        s_c1 = sem("s_c1")
        s_th = sem("s_th")
        s_mv = sem("s_mv")
        s_rstd1 = sem("s_rstd1")
        s_res = sem("s_res")
        s_xe = [sem(f"s_xe{i}") for i in range(2)]
        s_out = [sem(f"s_out{i}") for i in range(2)]

        def on_all(row):
            return row.broadcast_to([P, row.shape[-1]])

        def past(eng):
            eng.sem_inc(s_past, 1)

        def after(eng, semaphore, value):
            if not isinstance(value, int) or value > 0:
                eng.wait_ge(semaphore, value)

        def tile_of(m):
            first = SLOTS * TPB
            if isinstance(m, int) and m < NT - first:
                return first + m
            return m - (NT - first)

        def slot_of(s):
            if isinstance(s, int) and s < SPILL:
                return SLOTS - SPILL + s
            return s - SPILL

        def flat(ap):
            return ap.rearrange("p a n -> p (a n)")

        block = ctx.enter_context(nc.Block())

        @block.sync
        def _(sp):
            def raw_in(m):
                for q in range(4):
                    after(sp, s_conv, 4 * m + q - 3)
                    past(sp)
                    sp.dma_start(raw[:, q, :], adj[bass.ds(tile_of(m) * P, P), q * QUARTER:(q + 1) * QUARTER])\
                        .then_inc(s_raw[q], 16)

            def group_in(T, i):
                after(sp, s_xT, PACK * (T - 1))
                past(sp)
                sp.dma_start(xj[:, i, :], x[bass.ds(T * PACK * P, PACK * P), :]
                             .rearrange("(p b) d -> p (b d)", b=PACK)).then_inc(s_xj[i], 16)

            def group_out(T, i):
                sp.wait_ge(s_gst, PACK * (T + 1))
                past(sp)
                sp.dma_start(g_dram[bass.ds(T * PACK * P, PACK * P), :].rearrange("(p b) d -> p (b d)", b=PACK),
                             gst[:, i, :]).then_inc(s_gout[i], 16)

            group_in(0, 0)
            sp.dma_start(W0_sb[:, :, :], W0.rearrange("(c p) n -> p c n", p=P)).then_inc(s_w, 16)
            group_in(1, 1)
            sp.dma_start(Wsa_0[:, :, :], Wsa.rearrange("(c p) n -> p c n", p=P)).then_inc(s_w2, 16)
            for a in range(2):
                sp.dma_start(aB[:, a, :], on_all(asa[:, a * D:(a + 1) * D])).then_inc(s_w2, 16)
            raw_in(0)
            for a, v in enumerate((Wa, Wb)):
                sp.dma_start(VB[:, 2 + a, :], on_all(v[:, D:2 * D])).then_inc(s_w2, 16)
            sp.dma_start(b0B[:, :], on_all(b0.rearrange("(o n) -> o n", o=1))).then_inc(s_w2, 16)
            for a, v in enumerate((ba, bb)):
                sp.dma_start(gbias[:, a:a + 1], on_all(v.rearrange("(o n) -> o n", o=1))).then_inc(s_w2, 16)
            with sp.Fori(1, NG // 2) as pair:
                for i in range(2):
                    group_out(2 * pair + i - 2, i)
                    group_in(2 * pair + i, i)
            for i in range(2):
                group_out(NG - 2 + i, i)

            def tile_in(m, i):
                nt = tile_of(m)
                after(sp, s_x1, m - 1)
                past(sp)
                sp.dma_start(xres[:, i, :], x[bass.ds(nt * P, P), :]).then_inc(s_in[i], 16)
                sp.dma_start(gres[:, i, :], g_dram[bass.ds(nt * P, P), :]).then_inc(s_in[i], 16)

            def tile_out(m, i):
                nt = tile_of(m)
                sp.wait_ge(s_x1, m + 1)
                past(sp)
                sp.dma_start(x1_dram[bass.ds(nt * P, P), :], x1p[:, i, :].bitcast(F32)).then_inc(s_x1out[i], 16)
                sp.wait_ge(s_dots, m + 1)
                past(sp)
                for v, dram in enumerate((sl_dram, sr_dram)):
                    sp.dma_start(dram[bass.ds(nt * P, P), :], dots[:, bass.ds(nt, 1), v:v + 1]
                                 .rearrange("p a b -> p (a b)")).then_inc(s_slout, 16)

            def spill(k):
                sp.wait_ge(s_word, 2 * TPB * (k + 1))
                sp.dma_start(spill_dram[k], adjw[:, slot_of(k), :, :].rearrange("p a n -> p (a n)"))\
                    .then_inc(s_spill, 16)

            def stream(m, t):
                raw_in(m)
                if not isinstance(m, int) or m >= 5:
                    tile_out(m - 5, (t + 1) % 2)
                if not isinstance(m, int) or m >= 3:
                    tile_in(m - 3, (t + 1) % 2)
                for k in range(SPILL):
                    if isinstance(m, int) and m == TPB * (k + 1) + 2:
                        spill(k)

            for i in range(2):
                sp.wait_ge(s_gout[i], 16 * NG // 2)
            sp.wait_ge(s_prep, 9)
            for m in range(1, (SPILL + 2) * TPB):
                stream(m, m % TPB)
            with sp.Fori(SPILL + 2, NB) as s:
                for t in range(TPB):
                    stream(s * TPB + t, t)
            for m in range(NT, NT + 5):
                tile_out(m - 5, (m + 1) % 2)
                if m < NT + 3:
                    tile_in(m - 3, (m + 1) % 2)

            for i in range(2):
                sp.wait_ge(s_x1out[i], 16 * NT // 2)
            sp.wait_ge(s_slout, 32 * NT)
            sp.wait_ge(s_mm, UNITS * NT)

            def xs_in(group, T, i):
                after(sp, s_step, PACK * (group - XS_SLOTS + 1))
                past(sp)
                sp.dma_start(flat(xs[:, i, :, :]).bitcast(F32), x1_dram[bass.ds(T * PACK * P, PACK * P), :]
                             .rearrange("(p b) d -> p (b d)", b=PACK)).then_inc(s_xs[i], 16)

            def xe_in(nt, i):
                after(sp, s_mv, nt - 1)
                past(sp)
                sp.dma_start(xe[:, i, :], x1_dram[bass.ds(nt * P, P), :]).then_inc(s_xe[i], 16)

            def res_out(nt, i):
                sp.wait_ge(s_res, nt + 1)
                past(sp)
                sp.dma_start(out[bass.ds(nt * P, P), :], res[:, i, :]).then_inc(s_out[i], 16)

            sp.dma_start(srj[:, :].rearrange("p (t b) -> p t b", b=PACK),
                         sr_dram.rearrange("(t p b) o -> p t (b o)", p=P, b=PACK)).then_inc(s_srj, 16)
            sp.dma_start(slB[:, 0, :], on_all(sl_dram[0:CHUNK, :].rearrange("n o -> o n"))).then_inc(s_slB[0], 16)
            for i in range(XS_SLOTS):
                xs_in(i, i, i)
            sp.dma_start(slB[:, 1:NB, :], on_all(sl_dram[CHUNK:N, :].rearrange("n o -> o n"))
                         .rearrange("p (a n) -> p a n", n=CHUNK)).then_inc(s_slB[1], 16)
            sp.dma_start(Wsa_sb[:, :, :], Wsa.rearrange("(c p) n -> p c n", p=P)).then_inc(s_w3, 16)
            sp.dma_start(Wg_sb[:, :, 0:D], Wg.rearrange("(c p) n -> p c n", p=P)).then_inc(s_w3, 16)
            for a, v in enumerate((Wa, Wb)):
                sp.dma_start(Wg_sb[:, :, D + a:D + a + 1], v[0:1, 0:D].rearrange("o (c p) -> p c o", p=P),
                             allow_slow_non_contiguous=True).then_inc(s_w3, 16)
            sp.dma_start(bgB[:, :], on_all(bg.rearrange("(o n) -> o n", o=1))).then_inc(s_w3, 16)
            for T in range(XS_SLOTS, NG):
                xs_in(T, T, T % XS_SLOTS)

            def block_streams(p):
                g0 = p * NG + NG
                for T in range(NG):
                    xs_in(g0 + T, T, T % XS_SLOTS)
                    for t in range(TPB):
                        if T == (0 if t < 2 else (EPI[t - 2] + RESIDUAL) // PACK + 1):
                            xe_in(p * TPB + t, t % 2)
                        if T == min((EPI[t] + NORMED) // PACK + 1, NG - 1):
                            res_out(p * TPB + t, t % 2)

            def back(k):
                sp.wait_ge(s_af, NT * (k + 1))
                sp.dma_start(adjw[:, k, :, :].rearrange("p a n -> p (a n)"), spill_dram[k]).then_inc(s_back, 16)

            back(0)
            block_streams(0)
            back(1)
            with sp.Fori(1, NB - 1) as p:
                block_streams(p)
            for t in range(TPB):
                xe_in((NB - 1) * TPB + t, t % 2)
                if t > 0:
                    res_out((NB - 1) * TPB + t - 1, (t - 1) % 2)
            res_out(NT - 1, 1)
            for i in range(2):
                sp.wait_ge(s_out[i], 16 * NT // 2)

        @block.gpsimd
        def _(pool):
            pool.memset(ident[:, :], 0.0).then_inc(s_const, 1)
            pool.memset(ones[:, :], 1.0).then_inc(s_const, 1)
            for c, v in enumerate((-0.5, -1.0, EPS_NORM, 1.0)):
                pool.memset(consts[:, c:c + 1], v).then_inc(s_const, 1)
            pool.wait_ge(s_const, 6)
            pool.affine_select(out=ident[:, :], in_=ident[:, :], compare_op=ALU.not_equal, fill=1.0,
                               base=0, pattern=[[-1, P]], channel_multiplier=1).then_inc(s_const, 1)

            def degrees(m, t):
                i, d = t % 2, degs[:, t % 2, :]

                def link(ins, k):
                    ins.then_inc(s_rdeg, 1)
                    pool.wait_ge(s_rdeg, 5 * m + k)

                pool.wait_ge(s_conv, 4 * m + 4)
                after(pool, s_dots, m - 3)
                link(pool.tensor_tensor(d[:, 0:2], degq[:, i, 0:2], degq[:, i, 2:4], ALU.add), 1)
                link(pool.tensor_tensor(d[:, 2:3], d[:, 0:1], d[:, 1:2], ALU.add), 2)
                past(pool)
                link(pool.tensor_scalar(d[:, 3:4], d[:, 2:3], -ZERO * N, 1.0, ALU.add, ALU.max), 3)
                link(pool.tensor_tensor(rdeg[:, t, 0:1], d[:, 3:4], consts[:, 1:2], ALU.pow), 4)
                pool.tensor_tensor(rdeg[:, t, 1:2], rdeg[:, t, 0:1], consts[:, 3:4], ALU.add).then_inc(s_rdeg, 1)

            def norm_scale(i, seen, value, done, count):
                pool.wait_ge(seen, value)
                pool.tensor_tensor(vare[:, i:i + 1], mv[:, i, 1:2], consts[:, 2:3], ALU.add).then_inc(done, 1)
                pool.wait_ge(done, 2 * count + 1)
                pool.tensor_tensor(rstd[:, i:i + 1], vare[:, i:i + 1], consts[:, 0:1], ALU.pow).then_inc(done, 1)

            for m in range(TPB):
                degrees(m, m)
                if m >= 2:
                    norm_scale(m % 2, s_c0, TILE0 * (m - 2) + AGGR0, s_rstd0, m - 2)
            with pool.Fori(1, NB) as s:
                for t in range(TPB):
                    degrees(s * TPB + t, t)
                    norm_scale(t % 2, s_c0, TILE0 * (s * TPB + t - 2) + AGGR0, s_rstd0, s * TPB + t - 2)
            for m in range(NT - 2, NT):
                norm_scale(m % 2, s_c0, TILE0 * m + AGGR0, s_rstd0, m)

            def sum_step(n, k):
                if k == 0:
                    return
                pool.wait_ge(s_em, n + 1)
                if k > 1:
                    pool.wait_ge(s_rs, n)
                if k == 1:
                    after(pool, s_rs, n - 1)
                    pool.tensor_tensor(acc_first[:, :], em[:, 0, :], em[:, 1, :], ALU.add).then_inc(s_rs, 2)
                elif k < UNROLL:
                    pool.tensor_tensor(acc_first[:, :], acc_first[:, :], em[:, k % EM_SLOTS, :], ALU.add)\
                        .then_inc(s_rs, 1)
                elif k == UNROLL:
                    pool.tensor_tensor(acc[:, :], acc_first[:, :], em[:, 0, :], ALU.add).then_inc(s_rs, 1)
                else:
                    pool.tensor_tensor(acc[:, :], acc[:, :], em[:, k % EM_SLOTS, :], ALU.add).then_inc(s_rs, 1)

            for k in range(NT):
                sum_step(k, k)
            with pool.Fori(0, NB - 1) as p:
                for k in range(NT):
                    if k == UNROLL:
                        pool.wait_ge(s_denp, p + 1)
                    sum_step(p * NT + NT + k, k)
                    for t in range(TPB):
                        if k == EPI[t] + RESIDUAL:
                            norm_scale(t % 2, s_mv, p * TPB + t + 1, s_rstd1, p * TPB + t)
            for t in range(TPB):
                nt = (NB - 1) * TPB + t
                norm_scale(t % 2, s_mv, nt + 1, s_rstd1, nt)

        @block.scalar
        def _(act):
            def copy_xT(j, k):
                act.wait_ge(s_xT, j + 1)
                after(act, s_xw, j - 1)
                act.copy(xT[:, k % 2, :], xT_ps[k % 2][:, 0:D]).then_inc(s_xTc, 1)

            def copy_g(j, k):
                act.wait_ge(s_xw, j + 1)
                if k % PACK == 0:
                    after(act, s_gout[k // PACK], 2 * (j - k))
                act.copy(gst[:, k // PACK, (k % PACK) * D:(k % PACK + 1) * D], xw_ps[k % 2][:, 0:D])\
                    .then_inc(s_gst, 1)

            act.wait_ge(s_const, 7)
            copy_xT(0, 0)
            for k in range(1, 2 * PACK):
                copy_xT(k, k)
                copy_g(k - 1, k - 1)
            with act.Fori(1, NG // 2) as pair:
                for k in range(2 * PACK):
                    j = pair * (2 * PACK) + k
                    copy_xT(j, k)
                    copy_g(j - 1, (k - 1) % (2 * PACK))
            copy_g(NT - 1, 2 * PACK - 1)

            def to_bytes(m, t, q):
                act.wait_ge(s_raw[q], 16 * m + 16)
                if q == 0:
                    after(act, s_turn, 2 * m - 2)
                    after(act, s_rdeg, 5 * m - 5)
                past(act)
                act.activation(rowb[:, t % 2, q * QUARTER:(q + 1) * QUARTER], raw[:, q, :], ACT.Copy,
                               bias=ZERO, accum_out=degq[:, t % 2, q:q + 1]).then_inc(s_conv, 1)

            def copy_words(m, slot, t, h):
                act.wait_ge(s_turn, 2 * m + h + 1)
                act.copy(adjw[:, bass.ds(slot, 1), h * NG // 2:(h + 1) * NG // 2, t * P:(t + 1) * P]
                         .rearrange("p a g i -> p (a g) i"),
                         turned[h][:, :].rearrange("p (g i) -> p g i", i=P)).then_inc(s_word, 1)

            def tile(m, t, prev):
                for h in range(2):
                    to_bytes(m, t, 2 * h)
                    to_bytes(m, t, 2 * h + 1)
                    if not isinstance(m, int) or m > 0:
                        copy_words(m - 1, prev, (t - 1) % TPB, h)

            for s in range(SPILL + 1):
                for t in range(TPB):
                    tile(s * TPB + t, t, slot_of(s - 1 if t == 0 else s))
            act.wait_ge(s_spill, 16 * SPILL)
            with act.Fori(SPILL + 1, NB) as s:
                for t in range(TPB):
                    tile(s * TPB + t, t, slot_of(s - 1 if t == 0 else s))
            for h in range(2):
                copy_words(NT - 1, SLOTS - 1, TPB - 1, h)

            act.wait_ge(s_dots, NT)
            act.activation(esl[:, :], dots[:, :, 0], ACT.Exp, scale=SLOPE).then_inc(s_tabe, 1)
            act.wait_ge(s_srj, 16)
            act.activation(qsr[:, :], srj[:, :], ACT.Exp, scale=-SLOPE).then_inc(s_tabe, 1)
            act.wait_ge(s_tab, 1)
            act.wait_ge(s_mm, UNITS * NT)
            for i in range(2):
                act.wait_ge(s_x1out[i], 16 * NT // 2)

            def step(n, q, slot, T, k):
                b = k % PACK
                after(act, s_afu, n - AF_SLOTS + 1)
                chunk = adjw[:, bass.ds(slot, 1), bass.ds(T, 1), :].bitcast(U8)\
                    .rearrange("p a g (i b) -> p (a g i) b", b=PACK)[:, :, b]
                act.activation(af[:, k % AF_SLOTS, :], chunk, ACT.Copy, bias=-ZERO).then_inc(s_af, 1)
                act.activation(e1x[:, k % 2, :], flat(slB[:, bass.ds(q, 1), :]), ACT.Exp,
                               bias=nsr[:, bass.ds(T * PACK + b, 1)], scale=SLOPE - 1.0).then_inc(s_e1, 1)
                if not isinstance(n, int) or n > 0:
                    high(n, k)

            def high(n, k):
                act.wait_ge(s_em, n)
                after(act, s_step, n - EH_SLOTS)
                act.copy(ehi[:, (k - 1) % EH_SLOTS, :], em[:, (k - 1) % EM_SLOTS, :]).then_inc(s_ehi, 1)

            act.wait_ge(s_slB[0], 16)
            for k in range(UNROLL):
                step(k, 0, 0, k // PACK, k)
            with act.Fori(1, NT // UNROLL) as eight:
                for k in range(UNROLL):
                    step(eight * UNROLL + k, 0, 0, eight * (UNROLL // PACK) + k // PACK, k)
            act.wait_ge(s_slB[1], 16)

            def copy_A(count):
                act.wait_ge(s_afu, (count + 1) * NT)
                after(act, s_q, count * TPB)
                for c in range(KC):
                    act.copy(otA[:, c, :], accA[c][:, :]).then_inc(s_otA, 1)

            def gates(nt, i):
                act.wait_ge(s_lg, nt + 1)
                act.activation(eg[:, i, :], lg[:, i, :], ACT.Exp, scale=-1.0).then_inc(s_eg, 1)

            def tanh(nt, i):
                act.wait_ge(s_w1, nt + 1)
                act.activation(w[:, i, :], w[:, i, :], ACT.Tanh, scale=0.5).then_inc(s_th, 1)

            def block_steps(p, slot):
                n0 = p * NT + NT
                for k in range(NT):
                    step(n0 + k, p + 1, slot, k // PACK, k)
                    if k == AHEAD - 1:
                        copy_A(p)
                    for t in range(TPB):
                        if k == EPI[t] + GATES:
                            gates(p * TPB + t, t % 2)
                        if k == EPI[t] + TANH:
                            tanh(p * TPB + t, t % 2)

            block_steps(0, 1)
            with act.Fori(1, SLOTS - 1) as p:
                block_steps(p, p + 1)
            act.wait_ge(s_back, 16 * SPILL)
            with act.Fori(SLOTS - 1, NB - 1) as p:
                block_steps(p, p - (SLOTS - 1))
            high(NB * NT, 0)
            copy_A(NB - 1)
            for t in range(TPB):
                gates((NB - 1) * TPB + t, t % 2)
                tanh((NB - 1) * TPB + t, t % 2)

        @block.vector
        def _(dve):
            dve.wait_ge(s_w2, 16 * 8)
            for a in range(2):
                for c in range(KC):
                    after(dve, s_prep, 2 * a + c - 1)
                    dve.scalar_tensor_tensor(out=djunk[:, c, :], in0=Wsa_0[:, c, :], scalar=1.0,
                                             in1=aB[:, a, :], op0=ALU.mult, op1=ALU.mult,
                                             accum_out=lg[:, a, c:c + 1]).then_inc(s_prep, 1)
            dve.wait_ge(s_prep, 4)
            dve.wait_ge(s_const, 7)
            for a in range(2):
                for c in range(KC):
                    dve.tensor_scalar(diag[:, 2 * a + c, :], ident[:, :], lg[:, a, c:c + 1], None, ALU.mult)\
                        .then_inc(s_prep, 1)

            def g_parts(j, k):
                ps = xw_ps[k % 2][:, 0:D]
                dve.wait_ge(s_gst, j + 1)
                dve.tensor_copy(flat(G[:, bass.ds(j, 1), 0:D]), ps).then_inc(s_ghi, 1)
                dve.wait_ge(s_ghi, j + 1)
                dve.tensor_tensor(flat(G[:, bass.ds(j, 1), D:2 * D]), ps,
                                  flat(G[:, bass.ds(j, 1), 0:D]).bitcast(F32), ALU.subtract).then_inc(s_glo, 1)

            with dve.Fori(0, NT // 2) as pair:
                for k in range(2):
                    g_parts(2 * pair + k, k)
            dve.wait_ge(s_prep_pe, 1)
            dve.tensor_copy(VB[:, 0:2, :], prep_ps[:, :].rearrange("p (a n) -> p a n", a=2)).then_inc(s_prep, 1)
            dve.wait_ge(s_prep, 9)
            for i in range(2):
                dve.wait_ge(s_gout[i], 16 * NG // 2)

            def to_float(m, slot, t, unit):
                dve.wait_ge(s_word, 2 * m + unit // 2 + 1)
                after(dve, s_mm, UNITS * (m - 1) + unit + 1)
                g = JU // PACK
                dve.tensor_scalar(
                    af0[:, unit, :].rearrange("p (g b i) -> p g b i", g=g, b=PACK),
                    adjw[:, bass.ds(slot, 1), unit * g:(unit + 1) * g, t * P:(t + 1) * P].bitcast(U8)
                    .rearrange("p a g (i b) -> p (a g) b i", b=PACK),
                    -ZERO, None, ALU.add).then_inc(s_af0, 1)

            def sums_of(m, t):
                i, c = t % 2, m * TILE0
                ui, sums = u[:, i, :], bank[i]
                after(dve, s_dots, m - 1)
                dve.wait_ge(s_mm, UNITS * m + UNITS)
                dve.wait_ge(s_rdeg, 5 * m + 5)
                dve.scalar_tensor_tensor(out=ui, in0=sums[:, D:2 * D], scalar=rdeg[:, t, 0:1],
                                         in1=b0B[:, :], op0=ALU.mult, op1=ALU.add).then_inc(s_c0, 1)
                dve.wait_ge(s_c0, c + 1)
                dve.scalar_tensor_tensor(out=ui, in0=sums[:, 0:D], scalar=rdeg[:, t, 0:1], in1=ui,
                                         op0=ALU.mult, op1=ALU.add).then_inc(s_free0, 1)

            def own_terms(m, t):
                i, c = t % 2, m * TILE0
                ui = u[:, i, :]
                dve.wait_ge(s_in[i], 16 * (m - i) + 32)
                dve.wait_ge(s_free0, m + 1)
                dve.scalar_tensor_tensor(out=ui, in0=gres[:, i, :], scalar=rdeg[:, t, 1:2], in1=ui,
                                         op0=ALU.mult, op1=ALU.add).then_inc(s_c0, 1)
                dve.wait_ge(s_c0, c + 2)
                dve.scalar_tensor_tensor(out=ui, in0=ui, scalar=0.0, in1=xres[:, i, :],
                                         op0=ALU.max, op1=ALU.add).then_inc(s_c0, 1)

            def moments(m, t):
                i, c = t % 2, m * TILE0
                dve.wait_ge(s_c0, c + 3)
                dve.bn_stats(stats[:, i, :], u[:, i, :]).then_inc(s_c0, 1)
                dve.wait_ge(s_c0, c + 4)
                past(dve)
                dve.bn_aggr(mv[:, i, :], stats[:, i, :]).then_inc(s_c0, 1)

            def dot(m, t, v):
                if v == 1:
                    after(dve, s_dots, m)
                if v >= 2:
                    dve.wait_ge(s_c0, m * TILE0 + 6 + v)
                dve.scalar_tensor_tensor(
                    out=djunk[:, v % 2, :], in0=u[:, t % 2, :], scalar=1.0, in1=VB[:, v, :],
                    op0=ALU.mult, op1=ALU.mult,
                    accum_out=dots[:, bass.ds(tile_of(m), 1), v:v + 1].rearrange("p a b -> p (a b)"))\
                    .then_inc(s_c0 if v < 3 else s_dots, 1)

            def normed(m, t):
                i, c = t % 2, m * TILE0
                ui = u[:, i, :]
                dve.wait_ge(s_rstd0, 2 * m + 2)
                dve.tensor_scalar(ui, ui, mv[:, i, 0:1], rstd[:, i:i + 1], ALU.subtract, ALU.mult)\
                    .then_inc(s_c0, 1)
                after(dve, s_x1out[i], 8 * (m - i))
                dve.wait_ge(s_c0, c + 6)
                dve.tensor_copy(x1p[:, i, 0:D], ui).then_inc(s_c0, 1)
                dot(m, t, 0)
                dve.wait_ge(s_c0, c + 7)
                dve.tensor_tensor(x1p[:, i, D:2 * D], ui, x1p[:, i, 0:D].bitcast(F32), ALU.subtract)\
                    .then_inc(s_x1, 1)
                dot(m, t, 1)

            def tile(m, slot, t):
                e = (t - 2) % TPB
                sums_of(m - 2, e)
                own_terms(m - 2, e)
                to_float(m, slot, t, 0)
                moments(m - 2, e)
                to_float(m, slot, t, 1)
                normed(m - 2, e)
                to_float(m, slot, t, 2)
                dot(m - 2, e, 2)
                dot(m - 2, e, 3)
                to_float(m, slot, t, 3)

            for m in range(2):
                for unit in range(UNITS):
                    to_float(m, slot_of(0), m, unit)
            for m in range(2, (SPILL + 1) * TPB):
                tile(m, slot_of(m // TPB), m % TPB)
            with dve.Fori(SPILL + 1, NB) as s:
                for t in range(TPB):
                    tile(s * TPB + t, slot_of(s), t)
            for m in range(NT - 2, NT):
                sums_of(m, m % TPB)
                own_terms(m, m % TPB)
                moments(m, m % TPB)
                normed(m, m % TPB)
                dot(m, m % TPB, 2)
                dot(m, m % TPB, 3)

            dve.wait_ge(s_dots, NT)
            dve.wait_ge(s_srj, 16)
            dve.tensor_scalar(nsr[:, :], srj[:, :], -1.0, None, ALU.mult).then_inc(s_tab, 1)
            for a in range(2):
                dve.tensor_scalar(gatex[:, :, a], dots[:, :, 2 + a], gbias[:, a:a + 1], None, ALU.add)\
                    .then_inc(s_tab, 1)
            dve.wait_ge(s_tabe, 2)
            dve.tensor_scalar(epsrow[:, :], esl[:, :], EPS_SUM, None, ALU.mult).then_inc(s_tab, 1)
            dve.wait_ge(s_tab, 4)
            for i in range(2):
                dve.wait_ge(s_x1out[i], 16 * NT // 2)

            def step(n, T, k):
                dve.wait_ge(s_e1, n + 1)
                dve.wait_ge(s_af, n + 1)
                after(dve, s_elo, n - EM_SLOTS + 1)
                after(dve, s_rs, n - EM_SLOTS + 1)
                dve.scalar_tensor_tensor(out=em[:, k % EM_SLOTS, :], in0=e1x[:, k % 2, :],
                                         scalar=qsr[:, bass.ds(T * PACK + k % PACK, 1)],
                                         in1=af[:, k % AF_SLOTS, :].bitcast(F32),
                                         op0=ALU.min, op1=ALU.mult).then_inc(s_em, 1)
                if not isinstance(n, int) or n > 0:
                    low(n, k)

            def low(n, k):
                dve.wait_ge(s_ehi, n)
                after(dve, s_step, n - EH_SLOTS)
                dve.tensor_tensor(elo[:, (k - 1) % EH_SLOTS, :], em[:, (k - 1) % EM_SLOTS, :],
                                  ehi[:, (k - 1) % EH_SLOTS, :].bitcast(F32), ALU.subtract).then_inc(s_elo, 1)

            def copy_E(count):
                dve.wait_ge(s_step, (count + 1) * NT)
                after(dve, s_q, count * TPB)
                for c in range(KC):
                    dve.tensor_copy(otE[:, c, :], accE[c][:, :]).then_inc(s_otE, 1)

            def sums(count):
                dve.wait_ge(s_denp, count + 1)
                after(dve, s_w1, count * TPB)
                dve.tensor_tensor(den_sb[:, :], den_ps[:, DEN:DEN + TPB],
                                  epsrow[:, bass.ds(count * TPB, TPB)], ALU.add).then_inc(s_den, 1)

            def logits(nt, i):
                dve.wait_ge(s_q, nt + 1)
                dve.tensor_tensor(lg[:, i, :], qA[i][:, D:D + 2],
                                  gatex[:, bass.ds(nt, 1), :].rearrange("p a b -> p (a b)"), ALU.add)\
                    .then_inc(s_lg, 1)

            def gated_sum(p, nt, t):
                i, c = t % 2, [nt * TILE1]

                def link(ins):
                    ins.then_inc(s_c1, 1)
                    c[0] = c[0] + 1
                    dve.wait_ge(s_c1, c[0])

                dve.wait_ge(s_eg, nt + 1)
                dve.wait_ge(s_den, p + 1)
                link(dve.tensor_scalar(gc[:, i, :], eg[:, i, :], 1.0, None, ALU.add))
                link(dve.tensor_tensor(gc[:, i, 0:1], gc[:, i, 0:1], den_sb[:, t:t + 1], ALU.mult))
                link(dve.reciprocal(gr[:, i, :], gc[:, i, :]))
                link(dve.tensor_scalar(w[:, i, :], qE[i][:, 0:D], gr[:, i, 0:1], None, ALU.mult))
                dve.scalar_tensor_tensor(out=w[:, i, :], in0=qA[i][:, 0:D], scalar=gr[:, i, 1:2],
                                         in1=w[:, i, :], op0=ALU.mult, op1=ALU.add).then_inc(s_qr, 1)
                dve.wait_ge(s_qr, nt + 1)
                dve.scalar_tensor_tensor(out=w[:, i, :], in0=bgB[:, :], scalar=gr[:, i, 1:2],
                                         in1=w[:, i, :], op0=ALU.mult, op1=ALU.add).then_inc(s_w1, 1)

            def residual(p, nt, t):
                i, c = t % 2, [nt * TILE1 + 4]

                def link(ins):
                    ins.then_inc(s_c1, 1)
                    c[0] = c[0] + 1
                    dve.wait_ge(s_c1, c[0])

                dve.wait_ge(s_th, nt + 1)
                dve.wait_ge(s_xe[i], 32 * p + 16 * (t // 2) + 16)
                link(dve.scalar_tensor_tensor(out=r[:, i, :], in0=w[:, i, :], scalar=0.5, in1=xe[:, i, 0:D],
                                              op0=ALU.mult, op1=ALU.add))
                link(dve.scalar_tensor_tensor(out=r[:, i, :], in0=xe[:, i, D:2 * D], scalar=0.5, in1=r[:, i, :],
                                              op0=ALU.add, op1=ALU.add))
                link(dve.bn_stats(stats[:, i, :], r[:, i, :]))
                past(dve)
                dve.bn_aggr(mv[:, i, :], stats[:, i, :]).then_inc(s_mv, 1)

            def normalise(p, nt, t):
                i = t % 2
                dve.wait_ge(s_rstd1, 2 * nt + 2)
                after(dve, s_out[i], 32 * p + 16 * (t // 2))
                dve.tensor_scalar(res[:, i, :], r[:, i, :], mv[:, i, 0:1], rstd[:, i:i + 1],
                                  ALU.subtract, ALU.mult).then_inc(s_res, 1)

            for k in range(UNROLL):
                step(k, k // PACK, k)
            with dve.Fori(1, NT // UNROLL) as eight:
                for k in range(UNROLL):
                    step(eight * UNROLL + k, eight * (UNROLL // PACK) + k // PACK, k)
            dve.wait_ge(s_w3, 16 * 5)

            def block_steps(p):
                n0 = p * NT + NT
                for k in range(NT):
                    step(n0 + k, k // PACK, k)
                    if k == AHEAD - 1:
                        copy_E(p)
                    if k == AHEAD + 1:
                        sums(p)
                    for t in range(TPB):
                        nt = p * TPB + t
                        if k == EPI[t] + NORMED:
                            normalise(p, nt, t)
                        if k == EPI[t] + LOGITS:
                            logits(nt, t % 2)
                        if k == EPI[t] + GATED:
                            gated_sum(p, nt, t)
                        if k == EPI[t] + RESIDUAL:
                            residual(p, nt, t)

            block_steps(0)
            with dve.Fori(1, NB - 1) as p:
                block_steps(p)
            low(NB * NT, 0)
            copy_E(NB - 1)
            sums(NB - 1)
            for t in range(TPB):
                nt = (NB - 1) * TPB + t
                logits(nt, t % 2)
                gated_sum(NB - 1, nt, t)
                residual(NB - 1, nt, t)
                normalise(NB - 1, nt, t)

        @block.tensor
        def _(pe):
            pe.wait_ge(s_const, 7)

            def turn_x(j, group, k):
                if k % PACK == 0:
                    pe.wait_ge(s_xj[k // PACK], 16 * group + 16)
                after(pe, s_xTc, j - 1)
                for c in range(KC):
                    ins = pe.transpose(xT_ps[k % 2][:, c * P:(c + 1) * P],
                                       xj[:, k // PACK, (k % PACK) * D + c * P:(k % PACK) * D + (c + 1) * P],
                                       ident[:, :])
                ins.then_inc(s_xT, 1)

            def product(j, k):
                pe.wait_ge(s_xTc, j + 1)
                after(pe, s_glo, j - 1)
                for c in range(KC):
                    ins = pe.matmul(xw_ps[k % 2][:, 0:D], xT[:, k % 2, c * P:(c + 1) * P], W0_sb[:, c, :],
                                    start=(c == 0), stop=(c == KC - 1))
                ins.then_inc(s_xw, 1)

            turn_x(0, 0, 0)
            pe.wait_ge(s_w, 16)
            for k in range(1, 2 * PACK):
                turn_x(k, 0, k)
                product(k - 1, k - 1)
                if k == 3:
                    pe.wait_ge(s_prep, 8)
                    for v in range(4):
                        ins = pe.matmul(prep_ps[:, v * P:(v + 1) * P], ones[:, :], diag[:, v, :],
                                        start=True, stop=True)
                    ins.then_inc(s_prep_pe, 1)
            with pe.Fori(1, NG // 2) as pair:
                for k in range(2 * PACK):
                    turn_x(pair * (2 * PACK) + k, pair, k)
                    product(pair * (2 * PACK) + k - 1, k - 1)
            product(NT - 1, 1)

            def turn(m, i, h):
                words = rowb[:, i, :].bitcast(F32)
                pe.wait_ge(s_conv, 4 * m + 2 * h + 2)
                after(pe, s_word, 2 * m + h - 1)
                for g in range(NG // 2):
                    col = (h * NG // 2 + g) * P
                    ins = pe.transpose(turned[h][:, g * P:(g + 1) * P], words[:, col:col + P], ident[:, :])
                ins.then_inc(s_turn, 1)

            def sum_unit(m, i, unit):
                pe.wait_ge(s_af0, UNITS * m + unit + 1)
                if unit == 0:
                    after(pe, s_free0, m - 1)
                for j in range(JU):
                    ins = pe.matmul(bank[i][:, :], af0[:, unit, j * P:(j + 1) * P], G[:, unit * JU + j, :],
                                    start=(unit == 0 and j == 0), stop=(unit == UNITS - 1 and j == JU - 1))
                ins.then_inc(s_mm, 1)

            def tile(m, i):
                for h in range(2):
                    turn(m, i, h)
                    if not isinstance(m, int) or m > 0:
                        for unit in (2 * h, 2 * h + 1):
                            sum_unit(m - 1, (i - 1) % 2, unit)

            pe.wait_ge(s_prep, 9)
            pe.wait_ge(s_glo, NT)
            pe.wait_ge(s_ghi, NT)
            for m in range(2):
                tile(m, m)
            with pe.Fori(1, NT // 2) as pair:
                for i in range(2):
                    tile(2 * pair + i, i)
            for unit in range(UNITS):
                sum_unit(NT - 1, 1, unit)

            def step(n, k, landed, start, stop, p):
                i = k // PACK % XS_SLOTS
                tile = xs[:, i, k % PACK, :]
                hi = [tile[:, c * P:(c + 1) * P] for c in range(KC)]
                lo = [tile[:, D + c * P:D + (c + 1) * P] for c in range(KC)]
                if k % PACK == 0:
                    pe.wait_ge(s_xs[i], landed)
                pe.wait_ge(s_af, n + 1)
                a, eh, el = af[:, k % AF_SLOTS, :], ehi[:, k % EH_SLOTS, :], elo[:, k % EH_SLOTS, :]
                for c in range(KC):
                    if start and p is not None:
                        pe.wait_ge(s_otA, KC * p + c + 1)
                    pe.matmul(accA[c][:, :], hi[c], a, start=start, stop=False, skip_group_check=True)
                    ins = pe.matmul(accA[c][:, :], lo[c], a, start=False, stop=stop, skip_group_check=True)
                ins.then_inc(s_afu, 1)
                pe.wait_ge(s_ehi, n + 1)
                for c in range(KC):
                    if start and p is not None:
                        pe.wait_ge(s_otE, KC * p + c + 1)
                    pe.matmul(accE[c][:, :], hi[c], eh, start=start, stop=False, skip_group_check=True)
                    pe.matmul(accE[c][:, :], lo[c], eh, start=False, stop=False, skip_group_check=True)
                pe.wait_ge(s_elo, n + 1)
                for c in range(KC):
                    ins = pe.matmul(accE[c][:, :], hi[c], el, start=False, stop=stop, skip_group_check=True)
                ins.then_inc(s_step, 1)

            def row_sums(count):
                pe.wait_ge(s_rs, (count + 1) * NT)
                after(pe, s_qr, count * TPB)
                for t in range(TPB):
                    ins = pe.matmul(den_ps[:, DEN + t:DEN + t + 1], acc[:, t * P:(t + 1) * P], ones[:, 0:1],
                                    start=True, stop=True, skip_group_check=True)
                ins.then_inc(s_denp, 1)

            def weights(p, nt, t):
                i = t % 2
                if t == 0:
                    pe.wait_ge(s_otA, KC * p + KC)
                    pe.wait_ge(s_otE, KC * p + KC)
                if t == 1:
                    pe.wait_ge(s_den, p + 1)
                after(pe, s_qr, nt - 1)
                for c in range(KC):
                    pe.matmul(qE[i][:, 0:D], otE[:, c, t * P:(t + 1) * P], Wsa_sb[:, c, :],
                              start=(c == 0), stop=(c == KC - 1), skip_group_check=True)
                for c in range(KC):
                    ins = pe.matmul(qA[i][:, 0:D + 2], otA[:, c, t * P:(t + 1) * P], Wg_sb[:, c, :],
                                    start=(c == 0), stop=(c == KC - 1), skip_group_check=True)
                ins.then_inc(s_q, 1)

            per = 16 * NG // XS_SLOTS
            pe.wait_ge(s_free0, NT)
            pe.wait_ge(s_word, 2 * NT)
            for k in range(UNROLL):
                step(k, k, 16, k == 0, False, None)
            with pe.Fori(1, NT // UNROLL - 1) as eight:
                for k in range(UNROLL):
                    step(eight * UNROLL + k, k, 16 * eight + 16, False, False, None)
            for k in range(UNROLL):
                step(NT - UNROLL + k, k, per, False, k == UNROLL - 1, None)
            pe.wait_ge(s_w3, 16 * 5)

            def block_steps(p):
                n0, c0 = p * NT + NT, p * per + per
                for k in range(NT):
                    step(n0 + k, k, c0 + 16 * (k // UNROLL) + 16, k == 0, k == NT - 1, p)
                    if k == 0:
                        row_sums(p)
                    for t in range(TPB):
                        if k == EPI[t]:
                            weights(p, p * TPB + t, t)

            block_steps(0)
            with pe.Fori(1, NB - 1) as p:
                block_steps(p)
            row_sums(NB - 1)
            for t in range(TPB):
                weights(NB - 1, (NB - 1) * TPB + t, t)


_INS = ['x', 'adj', 'L0_gnn_W', 'L0_gnn_b', 'L1_gnn_W_sa', 'L1_gnn_a_sa', 'L1_gnn_W_gcnb', 'L1_gnn_b_gcnb',
        'L1_gnn_Wa', 'L1_gnn_ba', 'L1_gnn_Wb', 'L1_gnn_bb']
_OUTS = [((4096, 256), 'float32')]


def kernel(**inputs):
    import numpy as _np
    import concourse.bacc as _bacc
    from concourse import mybir as _mybir
    from concourse.bass_utils import run_bass_kernel_spmd as _run

    nc = _bacc.Bacc("TRN2", target_bir_lowering=False, num_devices=1, dynamic_dma_scratch_size=1024)
    arrays, args = {}, []
    for name in _INS:
        a = _np.ascontiguousarray(inputs[name])
        arrays[f"in_{name}_dram"] = a
        args.append(nc.dram_tensor(f"in_{name}_dram", a.shape, _mybir.dt.from_np(a.dtype), kind="ExternalInput").ap())
    for i, (shape, dtype) in enumerate(_OUTS):
        dt = _mybir.dt.from_np(_np.dtype(dtype))
        args.append(nc.dram_tensor(f"out_{i}_dram", shape, dt, kind="ExternalOutput").ap())
    two_layer_graph_kernel(nc, *args)
    r = _run(nc, [arrays], core_ids=[0])
    got = tuple(r.results[0][f"out_{i}_dram"] for i in range(len(_OUTS)))
    return got[0]
```

```python
from contextlib import ExitStack

import concourse.bass as bass
from concourse import mybir

ALU = mybir.AluOpType
ACT = mybir.ActivationFunctionType
F32 = mybir.dt.float32
F32R = mybir.dt.float32r
U8 = mybir.dt.uint8

P = 128
CHUNK = 512
TPB = CHUNK // P
PACK = 4
EPS_NORM = 1e-5
EPS_SUM = 1e-5
SLOPE = 0.01
ZERO = 48.0
SLOTS = 6
XS_SLOTS = 2
EM_SLOTS = 4
EH_SLOTS = 4
AF_SLOTS = 4
EPI = [2, 8, 14, 20]
LOGITS, GATES, GATED, TANH, RESIDUAL, NORMED = 5, 6, 7, 8, 9, 11
AHEAD = 4
FIRST_SUMS = 8
TILE0 = 10
AGGR0 = 5
TILE1 = 7
GATED_LINKS = 4


def two_layer_graph_kernel(nc, x, adj, W0, b0, Wsa, asa, Wg, bg, Wa, ba, Wb, bb, out):
    N, D = x.shape
    NT = N // P
    NB = N // CHUNK
    NG = NT // PACK
    KC = D // P
    QUARTER = N // 4
    SPILL = NB - SLOTS
    ROUND = XS_SLOTS * PACK
    UNITS = 4
    JU = NT // UNITS

    x1_dram = nc.dram_tensor("x1_parts", [N, 2 * D], F32, kind="Internal").ap()
    sl_dram = nc.dram_tensor("s_left", [N, 1], F32, kind="Internal").ap()
    sr_dram = nc.dram_tensor("s_right", [N, 1], F32, kind="Internal").ap()
    spill_dram = nc.dram_tensor("adj_spill", [SPILL, P, NG * CHUNK], F32, kind="Internal").ap()

    with ExitStack() as ctx:
        place = [(nc.sbuf_base + 31) // 32 * 32]

        def sb(name, shape, dt, at=None):
            size = mybir.dt.size(dt)
            for n in shape[1:]:
                size *= n
            size = (size + 31) // 32 * 32
            if at is None:
                at = place[0]
                place[0] += size
            assert at + size <= nc.sbuf_usable_end, (name, at + size - nc.sbuf_usable_end)
            return nc.alloc_sbuf_tensor_at(name, shape, dt, offset=at), at, at + size

        def keep(name, shape, dt):
            return sb(name, shape, dt)[0]

        def sem(name):
            return ctx.enter_context(nc.semaphore(name))

        adjw, a_adjw, _ = sb("adjw", [P, SLOTS, NG, CHUNK], F32)
        ident = keep("ident", [P, P], F32)
        srj = keep("srj", [P, NT], F32)
        nsr = keep("nsr", [P, NT], F32)
        qsr = keep("qsr", [P, NT], F32)
        degq = keep("degq", [P, 2, 4], F32)
        degs = keep("degs", [P, 2, 4], F32)
        rdeg = keep("rdeg", [P, 4, 2], F32)
        dots = keep("dots", [P, NT, 4], F32)
        consts = keep("consts", [P, 4], F32)
        gbias = keep("gbias", [P, 2], F32)
        stats = keep("stats", [P, 2, 6], F32)
        mv = keep("mv", [P, 2, 2], F32)
        vare = keep("vare", [P, 2], F32)
        rstd = keep("rstd", [P, 2], F32)
        lg = keep("lg", [P, 2, 2], F32)
        eg = keep("eg", [P, 2, 2], F32)
        gc = keep("gc", [P, 2, 2], F32)
        gr = keep("gr", [P, 2, 2], F32)
        den_sb = keep("den_sb", [P, TPB], F32)
        b0B = keep("b0B", [P, D], F32)
        VB = keep("VB", [P, 4, D], F32)

        X, a_X, _ = sb("X", [P, NT, 2 * D], F32R)
        X_in, _, _ = sb("X_in", [P, NT, 2 * D], F32, at=a_X)
        raw, a_raw, _ = sb("raw", [P, 4, QUARTER], F32)
        rowb, a_rowb, _ = sb("rowb", [P, 2, N], U8)
        af0, a_af0, _ = sb("af0", [P, UNITS, JU * P], F32R)
        W0s, a_W0s, _ = sb("W0s", [P, KC, 2 * D], F32R)
        W0_in, _, _ = sb("W0_in", [P, KC, 2 * D], F32, at=a_W0s)
        xres = keep("xres", [P, 4, D], F32)
        pl = keep("pl", [P, D], F32)
        pT_hi = keep("pT_hi", [P, D], F32R)
        pT_lo = keep("pT_lo", [P, D], F32R)
        u = keep("u", [P, D], F32)
        x1p = keep("x1p", [P, 2, 2 * D], F32R)
        unit_size = JU * 2 * D * mybir.dt.size(F32)
        xs, _, at = sb("xs", [P, XS_SLOTS, PACK, 2 * D], F32R, at=a_raw)
        assert at <= a_rowb
        slB0, _, at = sb("slB0", [P, CHUNK], F32, at=a_rowb)
        assert at <= a_af0
        af, _, at = sb("af", [P, AF_SLOTS, CHUNK], F32R, at=a_X)
        em, _, at = sb("em", [P, EM_SLOTS, CHUNK], F32, at=at)
        assert at <= a_X + unit_size
        ehi, _, at = sb("ehi", [P, EH_SLOTS, CHUNK], F32R, at=a_X + unit_size)
        elo, _, at = sb("elo", [P, EH_SLOTS, CHUNK], F32R, at=at)
        assert at <= a_X + 2 * unit_size
        slB, _, at = sb("slB", [P, NB - 1, CHUNK], F32, at=a_X + 2 * unit_size)
        acc, _, at = sb("acc", [P, CHUNK], F32, at=at)
        acc_first, _, at = sb("acc_first", [P, CHUNK], F32, at=at)
        xe, _, at = sb("xe", [P, 2, 2 * D], F32, at=at)
        w, _, at = sb("w", [P, 2, D], F32, at=at)
        r, _, at = sb("r", [P, 2, D], F32, at=at)
        res, _, at = sb("res", [P, 2, D], F32, at=at)
        esl, _, at = sb("esl", [P, NT], F32, at=at)
        epsrow, _, at = sb("epsrow", [P, NT], F32, at=at)
        gatex, _, at = sb("gatex", [P, NT, 2], F32, at=at)
        assert at <= a_raw
        place[0] = a_af0
        DG = D + 2

        def parts(name, n):
            whole, at, _ = sb(name, [P, KC, n], F32)
            return whole, keep(name + "_hi", [P, KC, n], F32R), sb(name + "_lo", [P, KC, n], F32R, at=at)[0]

        otA_hi, otA_lo, otE_hi, otE_lo = (keep(name, [P, KC, CHUNK], F32R)
                                          for name in ("otA_hi", "otA_lo", "otE_hi", "otE_lo"))
        Wsa_sb, Wsa_hi, Wsa_lo = parts("Wsa_sb", D)
        Wg_sb, Wg_hi, Wg_lo = parts("Wg_sb", DG)
        bgB = keep("bgB", [P, D], F32)
        late = a_adjw + 3 * NG * CHUNK * mybir.dt.size(F32)
        Wsa_0, _, at = sb("Wsa_0", [P, KC, D], F32, at=late)
        aB, _, at = sb("aB", [P, 2, D], F32, at=at)
        diag, _, at = sb("diag", [P, 4, P], F32, at=at)
        ones, _, _ = sb("ones", [P, P], F32, at=at)

        bank = [ctx.enter_context(nc.psum_tensor(f"bank{i}", [P, CHUNK], F32)) for i in range(8)]
        turned, pT_ps, y_ps, prep_ps = bank[2:4], bank[4], bank[5], bank[7]
        junk = bank[7][:, :].rearrange("p (a n) -> p a n", a=2)
        accA, accE = bank[2:4], bank[0:2]
        e1x = bank[6]
        qE, qA = [bank[4][:, 0:D], bank[4][:, D:2 * D]], [bank[5], bank[7]]
        qE_last = [bank[4][:, 0:D], bank[6][:, 0:D]]
        den_ps = bank[7]
        DEN = D + 4

        s_const = sem("s_const")
        s_past = sem("s_past")
        s_w = sem("s_w")
        s_w2 = sem("s_w2")
        s_w3 = sem("s_w3")
        s_prep = sem("s_prep")
        s_prep_pe = sem("s_prep_pe")
        s_xin = [sem(f"s_xin{i}") for i in range(NG)]
        s_hi = sem("s_hi")
        s_lo = sem("s_lo")
        s_raw = [sem(f"s_raw{i}") for i in range(4)]
        s_conv = sem("s_conv")
        s_rdeg = sem("s_rdeg")
        s_turn = sem("s_turn")
        s_word = sem("s_word")
        s_spill = sem("s_spill")
        s_af0 = sem("s_af0")
        s_mm = sem("s_mm")
        s_xr = sem("s_xr")
        s_pl = sem("s_pl")
        s_tp = sem("s_tp")
        s_pth = sem("s_pth")
        s_ptl = sem("s_ptl")
        s_y = sem("s_y")
        s_c0 = sem("s_c0")
        s_rstd0 = sem("s_rstd0")
        s_in = [sem(f"s_in{i}") for i in range(4)]
        s_x1 = sem("s_x1")
        s_dots = sem("s_dots")
        s_x1out = [sem(f"s_x1out{i}") for i in range(2)]
        s_slout = sem("s_slout")
        s_srj = sem("s_srj")
        s_tab = sem("s_tab")
        s_tabe = sem("s_tabe")
        s_slB = [sem(f"s_slB{i}") for i in range(2)]
        s_xs = [sem(f"s_xs{i}") for i in range(XS_SLOTS)]
        s_back = sem("s_back")
        s_af = sem("s_af")
        s_afu = sem("s_afu")
        s_e1 = sem("s_e1")
        s_em = sem("s_em")
        s_ehi = sem("s_ehi")
        s_elo = sem("s_elo")
        s_rs = sem("s_rs")
        s_step = sem("s_step")
        s_sum = sem("s_sum")
        s_oh = sem("s_oh")
        s_ol = sem("s_ol")
        s_denp = sem("s_denp")
        s_den = sem("s_den")
        s_q = sem("s_q")
        s_qr = sem("s_qr")
        s_lg = sem("s_lg")
        s_eg = sem("s_eg")
        s_w1 = sem("s_w1")
        s_c1 = sem("s_c1")
        s_th = sem("s_th")
        s_mv = sem("s_mv")
        s_rstd1 = sem("s_rstd1")
        s_res = sem("s_res")
        s_xe = [sem(f"s_xe{i}") for i in range(2)]
        s_out = [sem(f"s_out{i}") for i in range(2)]

        def on_all(row):
            return row.broadcast_to([P, row.shape[-1]])

        def past(eng):
            eng.sem_inc(s_past, 1)

        def after(eng, semaphore, value):
            if not isinstance(value, int) or value > 0:
                eng.wait_ge(semaphore, value)

        def tile_of(m):
            first = SLOTS * TPB
            if isinstance(m, int) and m < NT - first:
                return first + m
            return m - (NT - first)

        def slot_of(s):
            if isinstance(s, int) and s < SPILL:
                return SLOTS - SPILL + s
            return s - SPILL

        def group_of(s):
            return (s + SLOTS) % NG

        def columns(first, last):
            return slice(first * PACK, last * PACK)

        EARLY = ((0, NG - SPILL - 2), (NG - SPILL, NG))
        LATE = (NG - SPILL - 2, NG - SPILL)
        LATE_STEP = (NG - 2) * PACK - 8

        def there(m):
            return not isinstance(m, int) or 0 <= m < NT

        def flat(ap):
            return ap.rearrange("p a n -> p (a n)")

        block = ctx.enter_context(nc.Block())

        @block.sync
        def _(sp):
            def raw_in(m):
                for q in range(4):
                    after(sp, s_conv, 4 * m + q - 3)
                    past(sp)
                    sp.dma_start(raw[:, q, :], adj[bass.ds(tile_of(m) * P, P), q * QUARTER:(q + 1) * QUARTER])\
                        .then_inc(s_raw[q], 16)

            raw_in(0)
            for T in range(NG):
                sp.dma_start(X_in[:, T * PACK:(T + 1) * PACK, D:2 * D],
                             x[T * PACK * P:(T + 1) * PACK * P, :].rearrange("(p b) d -> p b d", b=PACK))\
                    .then_inc(s_xin[T], 16)
                if T == 1:
                    sp.dma_start(W0_in[:, :, D:2 * D], W0.rearrange("(c p) n -> p c n", p=P))\
                        .then_inc(s_w, 16)
            raw_in(1)
            sp.dma_start(Wsa_0[:, :, :], Wsa.rearrange("(c p) n -> p c n", p=P)).then_inc(s_w2, 16)
            for a in range(2):
                sp.dma_start(aB[:, a, :], on_all(asa[:, a * D:(a + 1) * D])).then_inc(s_w2, 16)
            for a, v in enumerate((Wa, Wb)):
                sp.dma_start(VB[:, 2 + a, :], on_all(v[:, D:2 * D])).then_inc(s_w2, 16)
            sp.dma_start(b0B[:, :], on_all(b0.rearrange("(o n) -> o n", o=1))).then_inc(s_w2, 16)
            for a, v in enumerate((ba, bb)):
                sp.dma_start(gbias[:, a:a + 1], on_all(v.rearrange("(o n) -> o n", o=1))).then_inc(s_w2, 16)

            def tile_in(m, i):
                nt = tile_of(m)
                after(sp, s_x1, m - 3)
                past(sp)
                sp.dma_start(xres[:, i, :], x[bass.ds(nt * P, P), :]).then_inc(s_in[i], 16)

            def tile_out(m, i):
                nt = tile_of(m)
                sp.wait_ge(s_x1, m + 1)
                past(sp)
                sp.dma_start(x1_dram[bass.ds(nt * P, P), :], x1p[:, i, :].bitcast(F32)).then_inc(s_x1out[i], 16)
                sp.wait_ge(s_dots, m + 1)
                past(sp)
                for v, dram in enumerate((sl_dram, sr_dram)):
                    sp.dma_start(dram[bass.ds(nt * P, P), :], dots[:, bass.ds(nt, 1), v:v + 1]
                                 .rearrange("p a b -> p (a b)")).then_inc(s_slout, 16)

            def spill(k):
                sp.wait_ge(s_word, 2 * TPB * (k + 1))
                sp.dma_start(spill_dram[k], adjw[:, slot_of(k), :, :].rearrange("p a n -> p (a n)"))\
                    .then_inc(s_spill, 16)

            def stream(m, t):
                if there(m):
                    raw_in(m)
                if there(m - 6):
                    tile_out(m - 6, t % 2)
                if there(m - 2):
                    tile_in(m - 2, (t - 2) % 4)
                for k in range(SPILL):
                    if isinstance(m, int) and m == TPB * (k + 1) + 2:
                        spill(k)

            for m in range(2, (SPILL + 2) * TPB):
                stream(m, m % TPB)
            with sp.Fori(SPILL + 2, NB) as s:
                for t in range(TPB):
                    stream(s * TPB + t, t)

            def xs_in(n, s):
                after(sp, s_step, PACK * (n - XS_SLOTS + 1))
                past(sp)
                T, i = group_of(s), s % XS_SLOTS
                sp.dma_start(flat(xs[:, i, :, :]).bitcast(F32), x1_dram[T * PACK * P:(T + 1) * PACK * P, :]
                             .rearrange("(p b) d -> p (b d)", b=PACK)).then_inc(s_xs[i], 16)

            def srj_in(first, last):
                sp.dma_start(srj[:, columns(first, last)].rearrange("p (t b) -> p t b", b=PACK),
                             sr_dram[first * PACK * P:last * PACK * P, :]
                             .rearrange("(t p b) o -> p t (b o)", p=P, b=PACK)).then_inc(s_srj, 16)

            def xe_in(nt, i):
                after(sp, s_mv, nt - 1)
                past(sp)
                sp.dma_start(xe[:, i, :], x1_dram[bass.ds(nt * P, P), :]).then_inc(s_xe[i], 16)

            def res_out(nt, i):
                sp.wait_ge(s_res, nt + 1)
                past(sp)
                sp.dma_start(out[bass.ds(nt * P, P), :], res[:, i, :]).then_inc(s_out[i], 16)

            ready = (NG - 2) * PACK
            stream(NT, 0)
            sp.wait_ge(s_slout, 32 * ready)
            for i in range(2):
                sp.wait_ge(s_x1out[i], 16 * ready // 2)
            for first, last in EARLY:
                srj_in(first, last)
            sp.wait_ge(s_conv, 4 * NT)
            for s in range(XS_SLOTS):
                xs_in(s, s)
            sp.wait_ge(s_turn, 2 * NT)
            sp.dma_start(slB0[:, :], on_all(sl_dram[0:CHUNK, :].rearrange("n o -> o n"))).then_inc(s_slB[0], 16)
            for m in range(NT + 1, NT + 6):
                if m >= NT + 4:
                    xs_in(m - NT - 2, m - NT - 2)
                stream(m, m % TPB)
            sp.wait_ge(s_slout, 32 * NT)
            for i in range(2):
                sp.wait_ge(s_x1out[i], 16 * NT // 2)
            srj_in(*LATE)
            sp.dma_start(slB[:, :, :], on_all(sl_dram[CHUNK:N, :].rearrange("n o -> o n"))
                         .rearrange("p (a n) -> p a n", n=CHUNK)).then_inc(s_slB[1], 16)
            sp.dma_start(Wsa_sb[:, :, :], Wsa.rearrange("(c p) n -> p c n", p=P)).then_inc(s_w3, 16)
            sp.dma_start(Wg_sb[:, :, 0:D], Wg.rearrange("(c p) n -> p c n", p=P)).then_inc(s_w3, 16)
            for a, v in enumerate((Wa, Wb)):
                sp.dma_start(Wg_sb[:, :, D + a:D + a + 1], v[0:1, 0:D].rearrange("o (c p) -> p c o", p=P),
                             allow_slow_non_contiguous=True).then_inc(s_w3, 16)
            sp.dma_start(bgB[:, :], on_all(bg.rearrange("(o n) -> o n", o=1))).then_inc(s_w3, 16)
            for s in range(4, NG):
                xs_in(s, s)

            def back(k):
                sp.wait_ge(s_af, NT * (k + 1))
                sp.dma_start(adjw[:, k, :, :].rearrange("p a n -> p (a n)"), spill_dram[k]).then_inc(s_back, 16)

            def block_streams(p, k):
                g0 = p * NG + NG
                for T in range(NG):
                    xs_in(g0 + T, T)
                    if T == 2 and k is not None:
                        back(k)
                    for t in range(TPB):
                        if T == (0 if t < 2 else (EPI[t - 2] + RESIDUAL) // PACK + 1):
                            xe_in(p * TPB + t, t % 2)
                        if T == min((EPI[t] + NORMED) // PACK + 1, NG - 1):
                            res_out(p * TPB + t, t % 2)

            for p in range(SPILL):
                block_streams(p, p)
            with sp.Fori(SPILL, NB - 1) as p:
                block_streams(p, None)
            last = (NB - 1) * TPB
            for t in range(TPB):
                xe_in(last + t, t % 2)
            for t in range(TPB):
                res_out(last + t, t % 2)
            for i in range(2):
                sp.wait_ge(s_out[i], 16 * NT // 2)

        @block.gpsimd
        def _(pool):
            pool.memset(ident[:, :], 0.0).then_inc(s_const, 1)
            pool.memset(ones[:, :], 1.0).then_inc(s_const, 1)
            for c, v in enumerate((-0.5, -1.0, EPS_NORM, 1.0)):
                pool.memset(consts[:, c:c + 1], v).then_inc(s_const, 1)
            pool.wait_ge(s_const, 6)
            pool.affine_select(out=ident[:, :], in_=ident[:, :], compare_op=ALU.not_equal, fill=1.0,
                               base=0, pattern=[[-1, P]], channel_multiplier=1).then_inc(s_const, 1)

            def degrees(m, t):
                i, d = t % 2, degs[:, t % 2, :]

                def link(ins, k):
                    ins.then_inc(s_rdeg, 1)
                    pool.wait_ge(s_rdeg, 5 * m + k)

                pool.wait_ge(s_conv, 4 * m + 4)
                after(pool, s_pl, 2 * (m - 3))
                link(pool.tensor_tensor(d[:, 0:2], degq[:, i, 0:2], degq[:, i, 2:4], ALU.add), 1)
                link(pool.tensor_tensor(d[:, 2:3], d[:, 0:1], d[:, 1:2], ALU.add), 2)
                past(pool)
                link(pool.tensor_scalar(d[:, 3:4], d[:, 2:3], -ZERO * N, 1.0, ALU.add, ALU.max), 3)
                link(pool.tensor_tensor(rdeg[:, t, 0:1], d[:, 3:4], consts[:, 1:2], ALU.pow), 4)
                pool.tensor_tensor(rdeg[:, t, 1:2], rdeg[:, t, 0:1], consts[:, 3:4], ALU.add).then_inc(s_rdeg, 1)

            def norm_scale(i, seen, value, done, count):
                pool.wait_ge(seen, value)
                pool.tensor_tensor(vare[:, i:i + 1], mv[:, i, 1:2], consts[:, 2:3], ALU.add).then_inc(done, 1)
                pool.wait_ge(done, 2 * count + 1)
                pool.tensor_tensor(rstd[:, i:i + 1], vare[:, i:i + 1], consts[:, 0:1], ALU.pow).then_inc(done, 1)

            def tile(m, t):
                if there(m):
                    degrees(m, t)
                if there(m - 3):
                    norm_scale((t - 3) % 2, s_c0, TILE0 * (m - 3) + AGGR0, s_rstd0, m - 3)

            for m in range(TPB):
                tile(m, m)
            with pool.Fori(1, NB) as s:
                for t in range(TPB):
                    tile(s * TPB + t, t)
            tile(NT, 0)

            def sum_step(n, k):
                if k == 0:
                    return
                pool.wait_ge(s_em, n + 1)
                if k > 1:
                    pool.wait_ge(s_rs, n)
                if k == 1:
                    after(pool, s_rs, n - 1)
                    pool.tensor_tensor(acc_first[:, :], em[:, 0, :], em[:, 1, :], ALU.add).then_inc(s_rs, 2)
                elif k < FIRST_SUMS:
                    pool.tensor_tensor(acc_first[:, :], acc_first[:, :], em[:, k % EM_SLOTS, :], ALU.add)\
                        .then_inc(s_rs, 1)
                elif k == FIRST_SUMS:
                    pool.tensor_tensor(acc[:, :], acc_first[:, :], em[:, 0, :], ALU.add).then_inc(s_rs, 1)
                else:
                    pool.tensor_tensor(acc[:, :], acc[:, :], em[:, k % EM_SLOTS, :], ALU.add).then_inc(s_rs, 1)

            pool.wait_ge(s_mm, UNITS * NT)
            for k in range(NT):
                sum_step(k, k)
                if k in (3, 6):
                    tile(NT + k // 3, k // 3)
            with pool.Fori(0, NB - 1) as p:
                for k in range(NT):
                    if k == FIRST_SUMS:
                        pool.wait_ge(s_denp, p + 1)
                    sum_step(p * NT + NT + k, k)
                    for t in range(TPB):
                        if k == EPI[t] + RESIDUAL:
                            norm_scale(t % 2, s_mv, p * TPB + t + 1, s_rstd1, p * TPB + t)
            for t in range(TPB):
                nt = (NB - 1) * TPB + t
                norm_scale(t % 2, s_mv, nt + 1, s_rstd1, nt)

        @block.scalar
        def _(act):
            def to_bytes(m, t, q):
                act.wait_ge(s_raw[q], 16 * m + 16)
                if q == 0:
                    after(act, s_turn, 2 * m - 2)
                    after(act, s_rdeg, 5 * m - 5)
                past(act)
                act.activation(rowb[:, t % 2, q * QUARTER:(q + 1) * QUARTER], raw[:, q, :], ACT.Copy,
                               bias=ZERO, accum_out=degq[:, t % 2, q:q + 1]).then_inc(s_conv, 1)

            def copy_words(m, slot, t, h):
                act.wait_ge(s_turn, 2 * m + h + 1)
                act.copy(adjw[:, bass.ds(slot, 1), h * NG // 2:(h + 1) * NG // 2, t * P:(t + 1) * P]
                         .rearrange("p a g i -> p (a g) i"),
                         turned[h][:, :].rearrange("p (g i) -> p g i", i=P)).then_inc(s_word, 1)

            def own_x(m, t):
                act.wait_ge(s_in[t], 4 * (m - t) + 16)
                act.wait_ge(s_rdeg, 5 * m + 5)
                after(act, s_tp, m)
                past(act)
                act.activation(pl[:, :], xres[:, t, :], ACT.Copy, scale=rdeg[:, t, 1:2]).then_inc(s_xr, 1)

            def pooled_high(m):
                act.wait_ge(s_tp, m + 1)
                after(act, s_y, m)
                act.copy(pT_hi[:, :], pT_ps[:, 0:D]).then_inc(s_pth, 1)

            def tile(m, t, prev):
                late = not isinstance(m, int) or m > 3
                if there(m):
                    to_bytes(m, t, 0)
                    to_bytes(m, t, 1)
                if there(m - 1) and late:
                    copy_words(m - 1, prev, (t - 1) % TPB, 0)
                if there(m):
                    to_bytes(m, t, 2)
                if there(m - 3) and late:
                    pooled_high(m - 3)
                if there(m):
                    to_bytes(m, t, 3)
                if there(m - 2):
                    own_x(m - 2, (t - 2) % TPB)
                if there(m - 1) and late:
                    copy_words(m - 1, prev, (t - 1) % TPB, 1)

            tile(0, 0, None)
            for h in range(2):
                copy_words(0, slot_of(0), 0, h)
            for T in range(NG):
                act.wait_ge(s_xin[T], 16)
                act.copy(X[:, T * PACK:(T + 1) * PACK, 0:D], X_in[:, T * PACK:(T + 1) * PACK, D:2 * D])\
                    .then_inc(s_hi, 1)
            act.wait_ge(s_w, 16)
            act.copy(W0s[:, :, 0:D], W0_in[:, :, D:2 * D]).then_inc(s_hi, 1)
            for s in range(SPILL + 1):
                if s == SPILL:
                    act.wait_ge(s_prep, 9)
                for t in range(1 if s == 0 else 0, TPB):
                    tile(s * TPB + t, t, slot_of(s - 1 if t == 0 else s))
                    if s == 0 and t in (1, 2):
                        for h in range(2):
                            copy_words(t, slot_of(0), t, h)
                        if t == 2:
                            pooled_high(0)
            act.wait_ge(s_spill, 16 * SPILL)
            with act.Fori(SPILL + 1, NB) as s:
                for t in range(TPB):
                    tile(s * TPB + t, t, slot_of(s - 1 if t == 0 else s))
            tile(NT, 0, SLOTS - 1)
            tile(NT + 1, 1, None)

            def tables(first, last):
                act.activation(qsr[:, columns(first, last)], srj[:, columns(first, last)], ACT.Exp, scale=-SLOPE)\
                    .then_inc(s_tabe, 1)

            def step(n, sl, slot, k):
                T, b = group_of(k // PACK), k % PACK
                after(act, s_afu, n - AF_SLOTS + 1)
                chunk = adjw[:, bass.ds(slot, 1), T:T + 1, :].bitcast(U8)\
                    .rearrange("p a g (i b) -> p (a g i) b", b=PACK)[:, :, b]
                act.activation(af[:, k % AF_SLOTS, :], chunk, ACT.Copy, bias=-ZERO).then_inc(s_af, 1)
                after(act, s_em, n)
                if not isinstance(n, int):
                    past(act)
                act.activation(e1x[:, :], sl, ACT.Exp, bias=nsr[:, T * PACK + b:T * PACK + b + 1],
                               scale=SLOPE - 1.0).then_inc(s_e1, 1)
                if not isinstance(n, int) or n > 0:
                    high(n, k)

            def high(n, k):
                act.wait_ge(s_em, n)
                after(act, s_step, n - EH_SLOTS)
                act.copy(ehi[:, (k - 1) % EH_SLOTS, :], em[:, (k - 1) % EM_SLOTS, :]).then_inc(s_ehi, 1)

            act.wait_ge(s_srj, 16 * len(EARLY))
            for first, last in EARLY:
                tables(first, last)
            act.wait_ge(s_tab, len(EARLY))
            act.wait_ge(s_slB[0], 16)
            act.wait_ge(s_mm, UNITS * (NT - 1) + 2)
            for k in range(NT):
                step(k, slB0[:, :], 0, k)
                if k == 2:
                    tile(NT + 2, 2, None)
                if k == LATE_STEP:
                    act.wait_ge(s_srj, 16 * (len(EARLY) + 1))
                    tables(*LATE)
                    act.wait_ge(s_dots, NT)
                    act.activation(esl[:, :], dots[:, :, 0], ACT.Exp, scale=SLOPE).then_inc(s_tabe, 1)
                    act.wait_ge(s_tab, len(EARLY) + 3)
            act.wait_ge(s_slB[1], 16)

            act.wait_ge(s_w3, 16 * 5)
            for whole, hi in ((Wsa_sb, Wsa_hi), (Wg_sb, Wg_hi)):
                act.copy(hi[:, :, :], whole[:, :, :]).then_inc(s_oh, 1)

            def high_parts(count):
                after(act, s_q, count * TPB)
                for c in range(KC):
                    if c == 0:
                        act.wait_ge(s_sum, 2 * count + 1)
                    else:
                        act.wait_ge(s_afu, (count + 1) * NT)
                    act.copy(otA_hi[:, c, :], accA[c][:, :]).then_inc(s_oh, 1)
                for c in range(KC):
                    if c == 0:
                        act.wait_ge(s_sum, 2 * count + 2)
                    else:
                        act.wait_ge(s_step, (count + 1) * NT)
                    act.copy(otE_hi[:, c, :], accE[c][:, :]).then_inc(s_oh, 1)

            def gates(nt, i):
                act.wait_ge(s_lg, nt + 1)
                act.activation(eg[:, i, :], lg[:, i, :], ACT.Exp, scale=-1.0).then_inc(s_eg, 1)

            def tanh(nt, i):
                act.wait_ge(s_w1, nt + 1)
                act.activation(w[:, i, :], w[:, i, :], ACT.Tanh, scale=0.5).then_inc(s_th, 1)

            def block_steps(p, slot):
                n0 = p * NT + NT
                for k in range(NT):
                    if k == AHEAD - 1:
                        high_parts(p)
                    step(n0 + k, flat(slB[:, bass.ds(p, 1), :]), slot, k)
                    for t in range(TPB):
                        if k == EPI[t] + GATES:
                            gates(p * TPB + t, t % 2)
                        if k == EPI[t] + TANH:
                            tanh(p * TPB + t, t % 2)

            block_steps(0, 1)
            with act.Fori(1, SLOTS - 1) as p:
                block_steps(p, p + 1)
            act.wait_ge(s_back, 16 * SPILL)
            with act.Fori(SLOTS - 1, NB - 1) as p:
                block_steps(p, p - (SLOTS - 1))
            high(NB * NT, 0)
            high_parts(NB - 1)
            for pair in range(0, TPB, 2):
                for t in (pair, pair + 1):
                    gates((NB - 1) * TPB + t, t % 2)
                for t in (pair, pair + 1):
                    tanh((NB - 1) * TPB + t, t % 2)

        @block.vector
        def _(dve):
            def low_part(parts, whole, g):
                dve.wait_ge(s_hi, g + 1)
                dve.tensor_tensor(parts[:, :, D:2 * D], whole[:, :, D:2 * D], parts[:, :, 0:D].bitcast(F32),
                                  ALU.subtract).then_inc(s_lo, 1)

            def vectors():
                dve.wait_ge(s_w2, 16 * 8)
                for a in range(2):
                    for c in range(KC):
                        after(dve, s_prep, 2 * a + c - 1)
                        dve.scalar_tensor_tensor(out=junk[:, c, :], in0=Wsa_0[:, c, :], scalar=1.0,
                                                 in1=aB[:, a, :], op0=ALU.mult, op1=ALU.mult,
                                                 accum_out=lg[:, a, c:c + 1]).then_inc(s_prep, 1)
                dve.wait_ge(s_prep, 4)
                dve.wait_ge(s_const, 7)
                for a in range(2):
                    for c in range(KC):
                        dve.tensor_scalar(diag[:, 2 * a + c, :], ident[:, :], lg[:, a, c:c + 1], None, ALU.mult)\
                            .then_inc(s_prep, 1)

            def to_float(m, slot, t, unit):
                dve.wait_ge(s_word, 2 * m + unit // 2 + 1)
                after(dve, s_mm, UNITS * (m - 1) + unit + 1)
                g = JU // PACK
                dve.tensor_scalar(
                    af0[:, unit, :].rearrange("p (g b i) -> p g b i", g=g, b=PACK),
                    adjw[:, bass.ds(slot, 1), unit * g:(unit + 1) * g, t * P:(t + 1) * P].bitcast(U8)
                    .rearrange("p a g (i b) -> p (a g) b i", b=PACK),
                    -ZERO, None, ALU.add).then_inc(s_af0, 1)

            def pooled(m, t):
                p, sums = pl[:, :], bank[t % 2]
                dve.wait_ge(s_mm, UNITS * m + UNITS)
                dve.wait_ge(s_xr, m + 1)
                dve.scalar_tensor_tensor(out=p, in0=sums[:, D:2 * D], scalar=rdeg[:, t, 0:1], in1=p,
                                         op0=ALU.mult, op1=ALU.add).then_inc(s_pl, 1)
                dve.wait_ge(s_pl, 2 * m + 1)
                dve.scalar_tensor_tensor(out=p, in0=sums[:, 0:D], scalar=rdeg[:, t, 0:1], in1=p,
                                         op0=ALU.mult, op1=ALU.add).then_inc(s_pl, 1)

            def pooled_low(m):
                dve.wait_ge(s_pth, m + 1)
                after(dve, s_y, m)
                dve.tensor_tensor(pT_lo[:, :], pT_ps[:, 0:D], pT_hi[:, :].bitcast(F32), ALU.subtract)\
                    .then_inc(s_ptl, 1)

            def relu(m, t):
                c, ui, y = m * TILE0, u[:, :], y_ps
                after(dve, s_dots, m)
                dve.wait_ge(s_y, m + 1)
                dve.tensor_tensor(ui, y[:, D:2 * D], b0B[:, :], ALU.add).then_inc(s_c0, 1)
                dve.wait_ge(s_c0, c + 1)
                dve.tensor_tensor(ui, y[:, 0:D], ui, ALU.add).then_inc(s_c0, 1)
                dve.wait_ge(s_in[t], 4 * (m - t) + 16)
                dve.wait_ge(s_c0, c + 2)
                dve.scalar_tensor_tensor(out=ui, in0=ui, scalar=0.0, in1=xres[:, t, :],
                                         op0=ALU.max, op1=ALU.add).then_inc(s_c0, 1)

            def moments(m, t):
                i, c = t % 2, m * TILE0
                dve.wait_ge(s_c0, c + 3)
                dve.bn_stats(stats[:, i, :], u[:, :]).then_inc(s_c0, 1)
                dve.wait_ge(s_c0, c + 4)
                past(dve)
                dve.bn_aggr(mv[:, i, :], stats[:, i, :]).then_inc(s_c0, 1)

            def dot(m, t, v):
                if v >= 2:
                    dve.wait_ge(s_c0, m * TILE0 + 6 + v)
                dve.scalar_tensor_tensor(
                    out=junk[:, v % 2, :], in0=u[:, :], scalar=1.0, in1=VB[:, v, :],
                    op0=ALU.mult, op1=ALU.mult,
                    accum_out=dots[:, bass.ds(tile_of(m), 1), v:v + 1].rearrange("p a b -> p (a b)"))\
                    .then_inc(s_c0 if v < 3 else s_dots, 1)

            def normed(m, t):
                i, c = t % 2, m * TILE0
                ui = u[:, :]
                dve.wait_ge(s_rstd0, 2 * m + 2)
                dve.tensor_scalar(ui, ui, mv[:, i, 0:1], rstd[:, i:i + 1], ALU.subtract, ALU.mult)\
                    .then_inc(s_c0, 1)
                after(dve, s_x1out[i], 8 * (m - i))
                dve.wait_ge(s_c0, c + 6)
                dve.tensor_copy(x1p[:, i, 0:D], ui).then_inc(s_c0, 1)
                dot(m, t, 0)
                dve.wait_ge(s_c0, c + 7)
                dve.tensor_tensor(x1p[:, i, D:2 * D], ui, x1p[:, i, 0:D].bitcast(F32), ALU.subtract)\
                    .then_inc(s_x1, 1)
                dot(m, t, 1)

            def tile(m, slot, t):
                a, e = (t - 2) % TPB, (t - 3) % TPB
                if there(m - 2):
                    pooled(m - 2, a)
                if there(m - 3):
                    relu(m - 3, e)
                if there(m):
                    to_float(m, slot, t, 0)
                if there(m - 3):
                    moments(m - 3, e)
                if there(m - 2):
                    pooled_low(m - 2)
                if there(m):
                    to_float(m, slot, t, 1)
                if there(m - 3):
                    normed(m - 3, e)
                if there(m):
                    to_float(m, slot, t, 2)
                if there(m - 3):
                    dot(m - 3, e, 2)
                    dot(m - 3, e, 3)
                if there(m):
                    to_float(m, slot, t, 3)

            tile(0, slot_of(0), 0)
            for T in range(NG):
                tiles = slice(T * PACK, (T + 1) * PACK)
                low_part(X[:, tiles, :], X_in[:, tiles, :], T)
            low_part(W0s[:, :, :], W0_in[:, :, :], NG)
            tile(1, slot_of(0), 1)
            vectors()
            tile(2, slot_of(0), 2)
            dve.wait_ge(s_prep_pe, 1)
            dve.tensor_copy(VB[:, 0:2, :], prep_ps[:, :].rearrange("p (a n) -> p a n", a=2)).then_inc(s_prep, 1)
            dve.wait_ge(s_prep, 9)
            for m in range(3, (SPILL + 1) * TPB):
                tile(m, slot_of(m // TPB), m % TPB)
            with dve.Fori(SPILL + 1, NB) as s:
                for t in range(TPB):
                    tile(s * TPB + t, slot_of(s), t)

            def tables(first, last):
                dve.tensor_scalar(nsr[:, columns(first, last)], srj[:, columns(first, last)], -1.0, None,
                                  ALU.mult).then_inc(s_tab, 1)

            def step(n, k):
                col = group_of(k // PACK) * PACK + k % PACK
                dve.wait_ge(s_e1, n + 1)
                dve.wait_ge(s_af, n + 1)
                after(dve, s_elo, n - EM_SLOTS + 1)
                after(dve, s_rs, n - EM_SLOTS + 1)
                dve.scalar_tensor_tensor(out=em[:, k % EM_SLOTS, :], in0=e1x[:, :],
                                         scalar=qsr[:, col:col + 1], in1=af[:, k % AF_SLOTS, :].bitcast(F32),
                                         op0=ALU.min, op1=ALU.mult).then_inc(s_em, 1)
                if not isinstance(n, int) or n > 0:
                    low(n, k)

            def low(n, k):
                dve.wait_ge(s_ehi, n)
                after(dve, s_step, n - EH_SLOTS)
                dve.tensor_tensor(elo[:, (k - 1) % EH_SLOTS, :], em[:, (k - 1) % EM_SLOTS, :],
                                  ehi[:, (k - 1) % EH_SLOTS, :].bitcast(F32), ALU.subtract).then_inc(s_elo, 1)

            def low_parts(count):
                banks = [*zip(accA, (otA_hi, ) * KC, (otA_lo, ) * KC), *zip(accE, (otE_hi, ) * KC, (otE_lo, ) * KC)]
                for k, (acc_ps, hi, lo) in enumerate(banks):
                    c = k % KC
                    dve.wait_ge(s_oh, 2 * KC * count + 3 + k)
                    dve.tensor_tensor(lo[:, c, :], acc_ps[:, :], hi[:, c, :].bitcast(F32), ALU.subtract)\
                        .then_inc(s_ol, 1)

            def sums(count):
                dve.wait_ge(s_denp, count + 1)
                after(dve, s_w1, count * TPB)
                dve.tensor_tensor(den_sb[:, :], den_ps[:, DEN:DEN + TPB],
                                  epsrow[:, bass.ds(count * TPB, TPB)], ALU.add).then_inc(s_den, 1)

            def logits(nt, i):
                dve.wait_ge(s_q, nt + 1)
                dve.tensor_tensor(lg[:, i, :], qA[i][:, D:DG],
                                  gatex[:, bass.ds(nt, 1), :].rearrange("p a b -> p (a b)"), ALU.add)\
                    .then_inc(s_lg, 1)

            def chained(start, side, stage, k):
                dve.wait_ge(s_c1, start + (stage - 1) * side + k + 1)

            def gated_sum(p, tiles, start, q=qE):
                side = len(tiles)
                for nt, t in tiles:
                    dve.wait_ge(s_eg, nt + 1)
                    dve.wait_ge(s_den, p + 1)
                    dve.tensor_scalar(gc[:, t % 2, :], eg[:, t % 2, :], 1.0, None, ALU.add).then_inc(s_c1, 1)
                for k, (nt, t) in enumerate(tiles):
                    chained(start, side, 1, k)
                    dve.tensor_tensor(gc[:, t % 2, 0:1], gc[:, t % 2, 0:1], den_sb[:, t:t + 1], ALU.mult)\
                        .then_inc(s_c1, 1)
                for k, (nt, t) in enumerate(tiles):
                    chained(start, side, 2, k)
                    dve.reciprocal(gr[:, t % 2, :], gc[:, t % 2, :]).then_inc(s_c1, 1)
                for k, (nt, t) in enumerate(tiles):
                    chained(start, side, 3, k)
                    dve.tensor_scalar(w[:, t % 2, :], q[t % 2], gr[:, t % 2, 0:1], None, ALU.mult)\
                        .then_inc(s_c1, 1)
                for k, (nt, t) in enumerate(tiles):
                    chained(start, side, 4, k)
                    dve.scalar_tensor_tensor(out=w[:, t % 2, :], in0=qA[t % 2][:, 0:D], scalar=gr[:, t % 2, 1:2],
                                             in1=w[:, t % 2, :], op0=ALU.mult, op1=ALU.add).then_inc(s_qr, 1)
                for nt, t in tiles:
                    dve.wait_ge(s_qr, nt + 1)
                    dve.scalar_tensor_tensor(out=w[:, t % 2, :], in0=bgB[:, :], scalar=gr[:, t % 2, 1:2],
                                             in1=w[:, t % 2, :], op0=ALU.mult, op1=ALU.add).then_inc(s_w1, 1)

            def residual(p, tiles, start):
                side = len(tiles)
                for nt, t in tiles:
                    i = t % 2
                    dve.wait_ge(s_th, nt + 1)
                    dve.wait_ge(s_xe[i], 32 * p + 16 * (t // 2) + 16)
                    dve.scalar_tensor_tensor(out=r[:, i, :], in0=w[:, i, :], scalar=0.5, in1=xe[:, i, 0:D],
                                             op0=ALU.mult, op1=ALU.add).then_inc(s_c1, 1)
                for k, (nt, t) in enumerate(tiles):
                    i = t % 2
                    chained(start, side, 1, k)
                    dve.scalar_tensor_tensor(out=r[:, i, :], in0=xe[:, i, D:2 * D], scalar=0.5, in1=r[:, i, :],
                                             op0=ALU.add, op1=ALU.add).then_inc(s_c1, 1)
                for k, (nt, t) in enumerate(tiles):
                    chained(start, side, 2, k)
                    dve.bn_stats(stats[:, t % 2, :], r[:, t % 2, :]).then_inc(s_c1, 1)
                for k, (nt, t) in enumerate(tiles):
                    chained(start, side, 3, k)
                    past(dve)
                    dve.bn_aggr(mv[:, t % 2, :], stats[:, t % 2, :]).then_inc(s_mv, 1)

            def normalise(p, nt, t):
                i = t % 2
                dve.wait_ge(s_rstd1, 2 * nt + 2)
                after(dve, s_out[i], 32 * p + 16 * (t // 2))
                dve.tensor_scalar(res[:, i, :], r[:, i, :], mv[:, i, 0:1], rstd[:, i:i + 1],
                                  ALU.subtract, ALU.mult).then_inc(s_res, 1)

            dve.wait_ge(s_srj, 16 * len(EARLY))
            for first, last in EARLY:
                tables(first, last)
            a, b = (NT - 2) % TPB, (NT - 1) % TPB
            pooled(NT - 2, a)
            relu(NT - 3, (NT - 3) % TPB)
            moments(NT - 3, (NT - 3) % TPB)
            pooled_low(NT - 2)
            dve.wait_ge(s_tabe, len(EARLY))
            step(0, 0)
            normed(NT - 3, (NT - 3) % TPB)
            pooled(NT - 1, b)
            step(1, 1)
            step(2, 2)
            pooled_low(NT - 1)
            step(3, 3)
            dot(NT - 3, (NT - 3) % TPB, 2)
            dot(NT - 3, (NT - 3) % TPB, 3)
            for k in range(4, NT):
                step(k, k)
                if k == 4:
                    relu(NT - 2, a)
                    moments(NT - 2, a)
                if k == 5:
                    normed(NT - 2, a)
                if k == 6:
                    dot(NT - 2, a, 2)
                    dot(NT - 2, a, 3)
                if k == 7:
                    relu(NT - 1, b)
                    moments(NT - 1, b)
                if k == 8:
                    normed(NT - 1, b)
                if k == 9:
                    dot(NT - 1, b, 2)
                    dot(NT - 1, b, 3)
                if k == LATE_STEP:
                    dve.wait_ge(s_srj, 16 * (len(EARLY) + 1))
                    tables(*LATE)
                    for a in range(2):
                        dve.wait_ge(s_dots, NT)
                        dve.tensor_scalar(gatex[:, :, a], dots[:, :, 2 + a], gbias[:, a:a + 1], None, ALU.add)\
                            .then_inc(s_tab, 1)
                    dve.wait_ge(s_tabe, len(EARLY) + 2)
                    dve.tensor_scalar(epsrow[:, :], esl[:, :], EPS_SUM, None, ALU.mult).then_inc(s_tab, 1)
            dve.wait_ge(s_tab, len(EARLY) + 4)
            dve.wait_ge(s_w3, 16 * 5)

            for k, (whole, hi, lo) in enumerate(((Wsa_sb, Wsa_hi, Wsa_lo), (Wg_sb, Wg_hi, Wg_lo))):
                dve.wait_ge(s_oh, k + 1)
                dve.tensor_tensor(lo[:, :, :], whole[:, :, :], hi[:, :, :].bitcast(F32), ALU.subtract)\
                    .then_inc(s_ol, 1)

            def block_steps(p):
                n0 = p * NT + NT
                for k in range(NT):
                    if k == AHEAD - 1:
                        low_parts(p)
                    step(n0 + k, k)
                    if k == AHEAD + 1:
                        sums(p)
                    for t in range(TPB):
                        nt = p * TPB + t
                        if k == EPI[t] + NORMED:
                            normalise(p, nt, t)
                        if k == EPI[t] + LOGITS:
                            logits(nt, t % 2)
                        if k == EPI[t] + GATED:
                            gated_sum(p, [(nt, t)], nt * TILE1)
                        if k == EPI[t] + RESIDUAL:
                            residual(p, [(nt, t)], nt * TILE1 + GATED_LINKS)

            block_steps(0)
            with dve.Fori(1, NB - 1) as p:
                block_steps(p)
            low(NB * NT, 0)
            sums(NB - 1)
            low_parts(NB - 1)
            last = (NB - 1) * TPB
            for t in range(0, TPB, 2):
                pair = [(last + t, t), (last + t + 1, t + 1)]
                for nt, t in pair:
                    logits(nt, t % 2)
                start = TILE1 * pair[0][0]
                gated_sum(NB - 1, pair, start, qE_last)
                residual(NB - 1, pair, start + 2 * GATED_LINKS)
                for nt, t in pair:
                    normalise(NB - 1, nt, t)

        @block.tensor
        def _(pe):
            pe.wait_ge(s_const, 7)

            def turn(m, i, h):
                words = rowb[:, i, :].bitcast(F32)
                pe.wait_ge(s_conv, 4 * m + 2 * h + 2)
                after(pe, s_word, 2 * m + h - 1)
                for g in range(NG // 2):
                    col = (h * NG // 2 + g) * P
                    ins = pe.transpose(turned[h][:, g * P:(g + 1) * P], words[:, col:col + P], ident[:, :])
                ins.then_inc(s_turn, 1)

            def sum_unit(m, i, unit):
                pe.wait_ge(s_af0, UNITS * m + unit + 1)
                if unit == 0:
                    after(pe, s_pl, 2 * (m - 1))
                if isinstance(m, int) and m == 0:
                    pe.wait_ge(s_lo, (unit + 1) * JU // PACK)
                for j in range(JU):
                    ins = pe.matmul(bank[i][:, :], af0[:, unit, j * P:(j + 1) * P], X[:, unit * JU + j, :],
                                    start=(unit == 0 and j == 0), stop=(unit == UNITS - 1 and j == JU - 1))
                ins.then_inc(s_mm, 1)

            def turn_pooled(m, i):
                pe.wait_ge(s_pl, 2 * m + 2)
                after(pe, s_ptl, m)
                for c in range(KC):
                    ins = pe.transpose(pT_ps[:, c * P:(c + 1) * P], pl[:, c * P:(c + 1) * P], ident[:, :])
                ins.then_inc(s_tp, 1)

            def product(m):
                pe.wait_ge(s_ptl, m + 1)
                after(pe, s_c0, TILE0 * (m - 1) + 2)
                for c in range(KC):
                    pe.matmul(y_ps[:, :], pT_hi[:, c * P:(c + 1) * P], W0s[:, c, :],
                              start=(c == 0), stop=False, skip_group_check=True)
                for c in range(KC):
                    ins = pe.matmul(y_ps[:, 0:D], pT_lo[:, c * P:(c + 1) * P], W0s[:, c, 0:D],
                                    start=False, stop=(c == KC - 1), skip_group_check=True)
                ins.then_inc(s_y, 1)

            def tile(m, i):
                for h in range(2):
                    if there(m):
                        turn(m, i, h)
                    for unit in (2 * h, 2 * h + 1):
                        if there(m - 1):
                            sum_unit(m - 1, (i - 1) % 2, unit)
                        if unit == 0 and there(m - 2):
                            turn_pooled(m - 2, i)
                if there(m - 2):
                    product(m - 2)

            tile(0, 0)
            for unit in range(UNITS):
                sum_unit(0, 0, unit)
            for h in range(2):
                turn(1, 1, h)
            for unit in range(UNITS):
                sum_unit(1, 1, unit)
            for h in range(2):
                turn(2, 0, h)
            pe.wait_ge(s_prep, 8)
            for v in range(4):
                ins = pe.matmul(prep_ps[:, v * P:(v + 1) * P], ones[:, :], diag[:, v, :], start=True, stop=True)
            ins.then_inc(s_prep_pe, 1)
            turn_pooled(0, 0)
            sum_unit(2, 0, 0)
            sum_unit(2, 0, 1)
            turn(3, 1, 0)
            pe.wait_ge(s_lo, NG + 1)
            product(0)
            sum_unit(2, 0, 2)
            turn_pooled(1, 1)
            sum_unit(2, 0, 3)
            turn(3, 1, 1)
            product(1)
            with pe.Fori(2, NT // 2) as pair:
                for i in range(2):
                    tile(2 * pair + i, i)
            tile(NT, NT % 2)

            def step(n, k, landed, start, stop, p):
                i = k // PACK % XS_SLOTS
                tile = xs[:, i, k % PACK, :]
                hi = [tile[:, c * P:(c + 1) * P] for c in range(KC)]
                lo = [tile[:, D + c * P:D + (c + 1) * P] for c in range(KC)]
                if k % PACK == 0:
                    pe.wait_ge(s_xs[i], landed)
                pe.wait_ge(s_af, n + 1)
                a, eh, el = af[:, k % AF_SLOTS, :], ehi[:, k % EH_SLOTS, :], elo[:, k % EH_SLOTS, :]
                for c in range(KC):
                    if start and p is not None:
                        pe.wait_ge(s_ol, 2 * KC * p + 3 + c)
                    pe.matmul(accA[c][:, :], hi[c], a, start=start, stop=False, skip_group_check=True)
                    ins = pe.matmul(accA[c][:, :], lo[c], a, start=False, stop=stop, skip_group_check=True)
                    if stop and c == 0:
                        ins.then_inc(s_sum, 1)
                ins.then_inc(s_afu, 1)
                pe.wait_ge(s_ehi, n + 1)
                for c in range(KC):
                    if start and p is not None:
                        pe.wait_ge(s_ol, 2 * KC * p + 3 + KC + c)
                    if start and p is None and c == 1:
                        pe.wait_ge(s_pl, 2 * NT)
                    pe.matmul(accE[c][:, :], hi[c], eh, start=start, stop=False, skip_group_check=True)
                    pe.matmul(accE[c][:, :], lo[c], eh, start=False, stop=False, skip_group_check=True)
                pe.wait_ge(s_elo, n + 1)
                for c in range(KC):
                    ins = pe.matmul(accE[c][:, :], hi[c], el, start=False, stop=stop, skip_group_check=True)
                    if stop and c == 0:
                        ins.then_inc(s_sum, 1)
                ins.then_inc(s_step, 1)

            def row_sums(count):
                pe.wait_ge(s_rs, (count + 1) * NT)
                after(pe, s_qr, count * TPB)
                for t in range(TPB):
                    ins = pe.matmul(den_ps[:, DEN + t:DEN + t + 1], acc[:, t * P:(t + 1) * P], consts[:, 3:4],
                                    start=True, stop=True, skip_group_check=True)
                ins.then_inc(s_denp, 1)

            def weights(p, nt, t, q=qE):
                i = t % 2
                if t == 0:
                    pe.wait_ge(s_ol, 2 * KC * p + 2 + 2 * KC)
                if t == 1:
                    pe.wait_ge(s_den, p + 1)
                after(pe, s_qr, nt if q is qE else nt - 1)
                for out_ps, n, a_hi, a_lo, w_hi, w_lo in ((q[i], D, otE_hi, otE_lo, Wsa_hi, Wsa_lo),
                                                          (qA[i], DG, otA_hi, otA_lo, Wg_hi, Wg_lo)):
                    for c in range(KC):
                        for a, b in ((a_hi, w_hi), (a_hi, w_lo), (a_lo, w_hi)):
                            ins = pe.matmul(out_ps[:, 0:n], a[:, c, t * P:(t + 1) * P], b[:, c, :],
                                            start=(c == 0 and b is w_hi and a is a_hi),
                                            stop=(c == KC - 1 and a is a_lo), skip_group_check=True)
                ins.then_inc(s_q, 1)

            per = 16 * NG // XS_SLOTS
            pe.wait_ge(s_word, 2 * NT)
            pe.wait_ge(s_pl, 2 * (NT - 1))
            for k in range(NT):
                if k == NT - 1:
                    row_sums(0)
                step(k, k, 16 * (k // ROUND) + 16, k == 0, k == NT - 1, None)
                if k == 0:
                    turn_pooled(NT - 1, (NT - 1) % 2)
                if k == 4:
                    product(NT - 1)
            pe.wait_ge(s_w3, 16 * 5)

            def block_steps(p):
                n0, c0 = p * NT + NT, p * per + per
                for k in range(NT):
                    if k == NT - 1:
                        row_sums(p + 1)
                    step(n0 + k, k, c0 + 16 * (k // ROUND) + 16, k == 0, k == NT - 1, p)
                    for t in range(TPB):
                        if k == EPI[t]:
                            weights(p, p * TPB + t, t)

            block_steps(0)
            with pe.Fori(1, NB - 1) as p:
                block_steps(p)
            for t in range(TPB):
                weights(NB - 1, (NB - 1) * TPB + t, t, qE_last)


_INS = ['x', 'adj', 'L0_gnn_W', 'L0_gnn_b', 'L1_gnn_W_sa', 'L1_gnn_a_sa', 'L1_gnn_W_gcnb', 'L1_gnn_b_gcnb',
        'L1_gnn_Wa', 'L1_gnn_ba', 'L1_gnn_Wb', 'L1_gnn_bb']
_OUTS = [((4096, 256), 'float32')]


def kernel(**inputs):
    import numpy as _np
    import concourse.bacc as _bacc
    from concourse import mybir as _mybir
    from concourse.bass_utils import run_bass_kernel_spmd as _run

    nc = _bacc.Bacc("TRN2", target_bir_lowering=False, num_devices=1, dynamic_dma_scratch_size=1024)
    arrays, args = {}, []
    for name in _INS:
        a = _np.ascontiguousarray(inputs[name])
        arrays[f"in_{name}_dram"] = a
        args.append(nc.dram_tensor(f"in_{name}_dram", a.shape, _mybir.dt.from_np(a.dtype), kind="ExternalInput").ap())
    for i, (shape, dtype) in enumerate(_OUTS):
        dt = _mybir.dt.from_np(_np.dtype(dtype))
        args.append(nc.dram_tensor(f"out_{i}_dram", shape, dt, kind="ExternalOutput").ap())
    two_layer_graph_kernel(nc, *args)
    r = _run(nc, [arrays], core_ids=[0])
    got = tuple(r.results[0][f"out_{i}_dram"] for i in range(len(_OUTS)))
    return got[0]
```
